# Optimizing a Trainium2 kernel written in Bass

```python
import numpy as np
import jax
import jax.numpy as jnp

def _softmax(x, axis=-1):
    return jax.nn.softmax(x, axis=axis)

def _gelu(x):
    return jax.nn.gelu(x, approximate=True)

def _silu(x):
    return jax.nn.silu(x)

def _sigmoid(x):
    return jax.nn.sigmoid(x)

def _layernorm(x, axis=-1, eps=1e-05):
    m = jnp.mean(x, axis=axis, keepdims=True)
    v = jnp.var(x, axis=axis, keepdims=True)
    return (x - m) / jnp.sqrt(v + eps)

def _scatter_add(tgt, idx, src, axis=0):
    return tgt.at[idx].add(src)

def _segment_sum(src, seg, n):
    return jax.ops.segment_sum(src, seg, n)
kernel_name = 'mk_xattn_ffn_d1_seqx_r8_90b915'

def setup_inputs(seed: int=0):
    np.random.seed(seed)
    _w = jnp.asarray

    def _rec_inputs():
        import jax
        import jax.numpy as jnp
        _rk = jax.random.key(seed)
        x = 7.22e-05 + 1 * jax.random.normal(jax.random.fold_in(_rk, 1), (2, 512, 128), jnp.float32)
        _lenS = 512 - jax.random.randint(jax.random.fold_in(_rk, 7), (2,), 0, max(1, 512 // 4) + 1, jnp.int32)
        _lenS2 = 77 - jax.random.randint(jax.random.fold_in(_rk, 8), (2,), 0, max(1, 77 // 4) + 1, jnp.int32)
        _ctx_1024P = jax.random.normal(jax.random.fold_in(_rk, 11), (2, 16, 128), jnp.float32)
        _ctx_1024c = jax.random.dirichlet(jax.random.fold_in(_rk, 511), 0.3 * jnp.ones((16,), jnp.float32), (2, 77))
        _ctx_1024t = jnp.einsum('bsk,bkd->bsd', _ctx_1024c, _ctx_1024P)
        _ctx_1024t = _ctx_1024t * jax.lax.rsqrt(jnp.mean(jnp.square(_ctx_1024t)) + 1e-12) * 0.953939
        ctx_1024 = 4.13588e-05 + 0.999923 * (_ctx_1024t + 0.3 * jax.random.normal(jax.random.fold_in(_rk, 611), (2, 77, 128), jnp.float32))
        return (x, ctx_1024)
    x, ctx_1024 = _rec_inputs()

    def _L0_xattn_setup():
        import jax, jax.numpy as jnp
        import numpy as np
        EMBED_DIM = 128
        NUM_HEADS = 16
        HEAD_DIM = EMBED_DIM // NUM_HEADS
        key = jax.random.key(seed)
        ks = jax.random.split(key, 12)
        B, S, D = (4, 256, EMBED_DIM)
        scale = 1.0 / np.sqrt(D)
        inp = {'query': jax.random.normal(ks[0], (B, S, D), jnp.float32), 'key': jax.random.normal(ks[1], (B, S, D), jnp.float32), 'value': jax.random.normal(ks[2], (B, S, D), jnp.float32), 'Wq': jax.random.normal(ks[3], (D, D), jnp.float32) * scale, 'bq': jnp.zeros((D,), jnp.float32), 'Wk': jax.random.normal(ks[4], (D, D), jnp.float32) * scale, 'bk': jnp.zeros((D,), jnp.float32), 'Wv': jax.random.normal(ks[5], (D, D), jnp.float32) * scale, 'bv': jnp.zeros((D,), jnp.float32), 'Wo': jax.random.normal(ks[6], (D, D), jnp.float32) * scale, 'bo': jnp.zeros((D,), jnp.float32)}
        return inp
    _L0_xattn_all = _L0_xattn_setup()
    _L0_xattn_in = {k: v for k, v in _L0_xattn_all.items() if k in ('Wq', 'bq', 'Wk', 'bk', 'Wv', 'bv', 'Wo', 'bo')}
    del _L0_xattn_all

    def _L0_ffn_setup():
        import jax, jax.numpy as jnp
        import numpy as np
        B, S, D = (4, 256, 128)
        E, F = (8, 512)
        key = jax.random.key(seed)
        ks = jax.random.split(key, 5)
        x = jax.random.normal(ks[0], (B, S, D), dtype=jnp.float32)
        switch_w = jax.random.normal(ks[1], (D, E), dtype=jnp.float32) * D ** (-0.5)
        switch_b = jnp.zeros((E,), dtype=jnp.float32)
        w1 = jax.random.normal(ks[2], (E, D, F), dtype=jnp.float32) * D ** (-0.5)
        b1 = jnp.zeros((E, F), dtype=jnp.float32)
        w2 = jax.random.normal(ks[3], (E, F, D), dtype=jnp.float32) * F ** (-0.5)
        b2 = jnp.zeros((E, D), dtype=jnp.float32)
        return {'x': x, 'switch_w': switch_w, 'switch_b': switch_b, 'w1': w1, 'b1': b1, 'w2': w2, 'b2': b2}
    _L0_ffn_all = _L0_ffn_setup()
    _L0_ffn_in = {k: v for k, v in _L0_ffn_all.items() if k in ('switch_w', 'switch_b', 'w1', 'b1', 'w2', 'b2')}
    del _L0_ffn_all
    return {'x': x, 'ctx_1024': ctx_1024, 'L0_xattn_Wq': _L0_xattn_in['Wq'], 'L0_xattn_bq': _L0_xattn_in['bq'], 'L0_xattn_Wk': _L0_xattn_in['Wk'], 'L0_xattn_bk': _L0_xattn_in['bk'], 'L0_xattn_Wv': _L0_xattn_in['Wv'], 'L0_xattn_bv': _L0_xattn_in['bv'], 'L0_xattn_Wo': _L0_xattn_in['Wo'], 'L0_xattn_bo': _L0_xattn_in['bo'], 'L0_ffn_switch_w': _L0_ffn_in['switch_w'], 'L0_ffn_switch_b': _L0_ffn_in['switch_b'], 'L0_ffn_w1': _L0_ffn_in['w1'], 'L0_ffn_b1': _L0_ffn_in['b1'], 'L0_ffn_w2': _L0_ffn_in['w2'], 'L0_ffn_b2': _L0_ffn_in['b2']}

def reference(x, ctx_1024, L0_xattn_Wq, L0_xattn_bq, L0_xattn_Wk, L0_xattn_bk, L0_xattn_Wv, L0_xattn_bv, L0_xattn_Wo, L0_xattn_bo, L0_ffn_switch_w, L0_ffn_switch_b, L0_ffn_w1, L0_ffn_b1, L0_ffn_w2, L0_ffn_b2):
    import jax
    import jax.numpy as jnp

    def _L0_xattn_ref(query, key, value, Wq, bq, Wk, bk, Wv, bv, Wo, bo):
        import jax, jax.numpy as jnp
        import numpy as np
        EMBED_DIM = 128
        NUM_HEADS = 16
        HEAD_DIM = EMBED_DIM // NUM_HEADS
        B, Sq, D = query.shape
        Sk = key.shape[1]
        H, Dh = (NUM_HEADS, HEAD_DIM)

        def proj(x, W, b):
            y = jnp.einsum('bsd,ed->bse', x, W) + b
            return y.reshape(x.shape[0], x.shape[1], H, Dh).transpose(0, 2, 1, 3)
        q = proj(query, Wq, bq)
        k = proj(key, Wk, bk)
        v = proj(value, Wv, bv)
        scores = jnp.einsum('bhqd,bhkd->bhqk', q, k) / jnp.sqrt(jnp.float32(Dh)).astype(q.dtype)
        attn = jax.nn.sigmoid(scores)
        out = jnp.einsum('bhqk,bhkd->bhqd', attn, v)
        out = out.transpose(0, 2, 1, 3).reshape(B, Sq, D)
        return jnp.einsum('bsd,ed->bse', out, Wo) + bo

    def _L0_ffn_ref(x, switch_w, switch_b, w1, b1, w2, b2):
        import jax, jax.numpy as jnp
        import numpy as np
        B, S, D = (4, 256, 128)
        E, F = (8, 512)
        b, s, d = x.shape
        t = x.reshape(-1, d)
        logits = t @ switch_w + switch_b
        route_prob = jax.nn.softmax(logits, axis=-1)
        route_prob_max = jnp.max(route_prob, axis=-1)
        routes = jnp.argmax(route_prob, axis=-1)
        out = jnp.zeros_like(t)
        n_experts = w1.shape[0]
        for e in range(n_experts):
            h = jax.nn.gelu(t @ w1[e] + b1[e])
            y = h @ w2[e] + b2[e]
            mask = (routes == e)[:, None]
            out = jnp.where(mask, y, out)
        out = out * route_prob_max[:, None]
        return out.reshape(b, s, d)
    x = x + _L0_xattn_ref(_layernorm(x, axis=-1), ctx_1024, ctx_1024, L0_xattn_Wq, L0_xattn_bq, L0_xattn_Wk, L0_xattn_bk, L0_xattn_Wv, L0_xattn_bv, L0_xattn_Wo, L0_xattn_bo)
    x = x + _L0_ffn_ref(_layernorm(x, axis=-1), L0_ffn_switch_w, L0_ffn_switch_b, L0_ffn_w1, L0_ffn_b1, L0_ffn_w2, L0_ffn_b2)
    return x

_drawn_inputs = setup_inputs


def setup_inputs(seed=0):
    import zlib

    import numpy as np

    out = dict(_drawn_inputs(seed))
    spreads = {'L0_xattn_bq': (0.0, 0.275),
     'L0_xattn_bk': (0.0, 0.1),
     'L0_xattn_bv': (0.0, 0.1),
     'L0_xattn_bo': (0.0, 0.8),
     'L0_ffn_switch_b': (0.0, 0.8),
     'L0_ffn_b1': (0.0, 0.8),
     'L0_ffn_b2': (0.0, 2.0)}
    factors = {'L0_ffn_switch_w': 4.611, 'L0_ffn_w1': 4.791, 'L0_ffn_w2': 4.31}
    for name, (base, spread) in spreads.items():
        noise = np.random.default_rng([zlib.crc32(name.encode()), seed]).standard_normal(out[name].shape)
        drawn = base * np.exp(spread * noise) if base else spread * noise
        out[name] = jnp.asarray(drawn.astype(out[name].dtype))
    for name, factor in factors.items():
        out[name] = (out[name] * factor).astype(out[name].dtype)
    return out
```

```python
from contextlib import ExitStack

import numpy as np

import concourse.bass as bass
from concourse import mybir

P = 128
B, S, D = 2, 512, 128
SK = 77
H, DH = 16, 8
E, F = 8, 512
NTOK = B * S
C = NTOK // P
CB = S // P
G = 4
GD = D // G
HG = H // G
KT = 3
KR = -(-HG * SK // KT)
KC = KT * KR
FC = F // P
NX = C - 1
NT = E + NX
W1, W2 = 0, F
WB = 2 * F
WCOLS = 2 * F + FC
MEAN, RSTD, PROB, TOK = D, D + 1, D + 2, D + 3
ROW = D + 4
EPS = 1e-5

IDENT, UPPER, ONES = 0, P, 2 * P
SEL_HI = 3 * P
SEL_LO = SEL_HI + G * P
VMASK = SEL_LO + G * P
KMASK = VMASK + KT * P
DESC = KMASK + HG
TRI = DESC + E
THRESH = TRI + E * E
JUMP = THRESH + NX
BASE = JUMP + E
TILE_NO = BASE + E
NCONST = TILE_NO + NX


def constants():
    t = np.zeros((P, NCONST), np.float32)
    p = np.arange(P)
    t[:, IDENT:IDENT + P] = np.eye(P)
    t[:, UPPER:UPPER + P] = p[:, None] < p[None, :]
    t[:, ONES:ONES + P] = 1
    for g in range(G):
        for m in range(P):
            at = SEL_HI if m < 2 * GD else SEL_LO
            t[g * GD + m % GD, at + g * P + m] = 1
    for k in range(KT):
        for r in range(KR):
            key = k * KR + r
            if key < HG * SK:
                t[r, VMASK + k * P:VMASK + (k + 1) * P] = (p % GD) // DH == key // SK
    for h in range(HG):
        t[:, KMASK + h] = (p % GD) // DH == h
    e = np.arange(E)
    t[:, DESC:DESC + E] = E - e
    t[:, TRI:TRI + E * E] = (e[None, :] < e[:, None]).reshape(-1)
    t[:, THRESH:THRESH + NX] = P * (1 + np.arange(NX))
    t[:, JUMP:JUMP + E] = (E - 1) * P - P * e
    t[:, BASE:BASE + E] = P * e
    t[:, TILE_NO:TILE_NO + NX] = np.arange(NX)
    return t


def build_program(nc, x, wk4, ctx_t, bk4, w_qvo, rows_1, const, weights, b2, out):
    F32, F32R, BF16, I32 = mybir.dt.float32, mybir.dt.float32r, mybir.dt.bfloat16, mybir.dt.int32
    ALU, ACT, AX = mybir.AluOpType, mybir.ActivationFunctionType, mybir.AxisListType.X
    ctx = ExitStack()
    with ctx:
        def sb(name, shape, dt=F32):
            return ctx.enter_context(nc.sbuf_tensor(name, shape, dt))

        def sem(name):
            return ctx.enter_context(nc.semaphore(name))

        x_sb = sb("x_sb", [P, C, D])
        cst = sb("cst", [P, NCONST])
        wk_sb = sb("wk_sb", [P, D])
        wkrep = sb("wkrep", [P, G, 4, GD])
        bk_sb = sb("bk_sb", [P, G + 1])
        ctx_sb = sb("ctx_sb", [P, B, SK])
        ctxrep = sb("ctxrep", [P, B, KC])
        wq_sb = sb("wq_sb", [P, 3 * D + E])
        brow = sb("brow", [P, 2 * D + E])
        bvm = sb("bvm", [KR, KT, P])
        sel = sb("sel", [P, 2 * G * P], F32R)
        tri_bf = sb("tri_bf", [P, 2 * P], BF16)
        half = sb("half", [P, C])
        stats = sb("stats", [P, C, 6])
        ln1 = sb("ln1", [P, C, 2])
        var_eps = sb("var_eps", [P, C])
        rstd1 = sb("rstd1", [P, C])
        xn = sb("xn", [P, C, D])
        xnT = sb("xnT", [P, B, S])
        q_part = sb("q_part", [P, B, 2, S], F32R)
        q_stack = sb("q_stack", [P, B, G, S], F32R)
        kf = sb("kf", [P, 2, 2 * B * SK])
        kpart = sb("kpart", [P, G, B * SK], F32R)
        kblk = sb("kblk", [P, B, G, KC], F32R)
        vtmp = sb("vtmp", [KR, B, KT * P])
        vblk = sb("vblk", [KR, B, KT, P])
        shared = sb("shared", [P, B * KT * G * S])
        probs = shared[0:KR, :].rearrange("p (b t g s) -> p b t g s", b=B, t=KT, g=G)
        attT = sb("attT", [P, B, S])
        rows = sb("rows", [P, C, ROW])
        xn2T = xnT
        logit = sb("logit", [P, C, E])
        lmax = sb("lmax", [P, C])
        lsub = sb("lsub", [P, C, E])
        lexp = sb("lexp", [P, C, E])
        lsum = sb("lsum", [P, C])
        eq = sb("eq", [P, C, E])
        first = sb("first", [P, C])
        chosen = sb("chosen", [P, C, E], BF16)
        over = sb("over", [P, E, NX])
        extra = sb("extra", [P, E])
        before = sb("before", [P, E, E])
        opened = sb("opened", [P, E])
        jump = sb("jump", [P, E])
        slot8 = sb("slot8", [P, C, E])
        slot = sb("slot", [P, C], I32)
        upto = sb("upto", [1, E])
        cmp_t = sb("cmp_t", [1, NX, E])
        owner_f = sb("owner_f", [1, NX])
        owner = sb("owner", [1, NX], I32)
        blank = sb("blank", [P, ROW])
        w_sb = sb("w_sb", [P, NT, WCOLS])
        hT = shared[:, NT * (ROW + 3 * D + P):NT * (ROW + 3 * D + P) + 3 * F].rearrange("p (i n) -> p i n", i=3)
        b2_sb = sb("b2_sb", [P, NT, D])
        srow, sxn, sxnT, y_sb, o_sb = (
            shared[:, NT * at:NT * (at + n)].rearrange("p (i n) -> p i n", i=NT)
            for at, n in ((0, ROW), (ROW, D), (ROW + D, P), (ROW + D + P, D), (ROW + 2 * D + P, D)))

        pair = [ctx.enter_context(nc.psum_tensor(f"pair{i}", [P, 2, 512], F32)) for i in range(2)]
        bank = [ctx.enter_context(nc.psum_tensor(f"bank{i}", [P, 512], F32)) for i in range(4)]
        k_ps, v_ps = pair[0], pair[1]
        xT_ps = [bank[0], bank[1]]
        q_ps = bank[2]
        stack_ps = [bank[0], bank[3]]
        att_ps = [bank[1], bank[2]]
        y_ps = [bank[0], bank[3]]
        x2T_ps = [bank[1], bank[2]]
        logit_ps = [bank[0], bank[3]]
        rank_ps = pair[0][:, 0, 0:C * E]
        count_ps = pair[0][:, 0, C * E:C * E + E]
        h_ps = [pair[1][:, 0, :], pair[1][:, 1, :]]
        t_ps = [bank[0], bank[1]]
        f_ps = [bank[2], bank[3]]

        slots_dram = nc.dram_tensor("slots_dram", (NT * P, ROW), F32).ap()

        x_in = [sem(f"x_in{b}") for b in range(B)]
        kv_in, qo_in, cst_in, brow_in = sem("kv_in"), sem("qo_in"), sem("cst_in"), sem("brow_in")
        w_in, wx_in, b2_in = sem("w_in"), sem("wx_in"), sem("b2_in")
        blank_ok, blanked, sent, srow_in, stored = (sem("blank_ok"), sem("blanked"), sem("sent"),
                                                    [sem(f"srow_in{i}") for i in range(3)], sem("stored"))
        pool_step, dve_step, act_step = sem("pool_step"), sem("dve_step"), sem("act_step")
        half_ok = sem("half_ok")
        wkrep_ok, ctxrep_ok, bvm_ok, tri_ok, sel_ok = (sem("wkrep_ok"), sem("ctxrep_ok"), sem("bvm_ok"),
                                                       sem("tri_ok"), sem("sel_ok"))
        aggr_ok, rstd_ok, xn_ok, xT_ok, xT_copied = (sem("aggr_ok"), sem("rstd_ok"), sem("xn_ok"),
                                                     sem("xT_ok"), sem("xT_copied"))
        xb_ok, tok_ok = sem("xb_ok"), sem("tok_ok")
        k_ok, k_read, kblk_ok, v_ok, v_read, vblk_ok = (sem("k_ok"), sem("k_read"), sem("kblk_ok"),
                                                        sem("v_ok"), sem("v_read"), sem("vblk_ok"))
        q_ok, qhi_ok, qlo_ok, stack_ok, stacked = (sem("q_ok"), sem("qhi_ok"), sem("qlo_ok"),
                                                   sem("stack_ok"), sem("stacked"))
        score_ok, prob_ok, att_ok, att_copied = sem("score_ok"), sem("prob_ok"), sem("att_ok"), sem("att_copied")
        y_ok, x1_ok, aggr2_ok, rstd2_ok, xn2_ok = (sem("y_ok"), sem("x1_ok"), sem("aggr2_ok"),
                                                   sem("rstd2_ok"), sem("xn2_ok"))
        x2T_ok, x2T_copied, logit_ok, lsub_ok, lexp_ok = (sem("x2T_ok"), sem("x2T_copied"), sem("logit_ok"),
                                                          sem("lsub_ok"), sem("lexp_ok"))
        logit_read, chosen_ok, rank_ok, slot_ok, owner_ok, prob_row_ok = (
            sem("logit_read"), sem("chosen_ok"), sem("rank_ok"), sem("slot_ok"), sem("owner_ok"), sem("prob_row_ok"))
        sxn_ok, sT_ok, sT_copied, h_ok, gelu_ok, f_ok, f_read, o_ok = (
            sem("sxn_ok"), sem("sT_ok"), sem("sT_copied"), sem("h_ok"), sem("gelu_ok"), sem("f_ok"),
            sem("f_read"), sem("o_ok"))

        units = [(b, t, pr) for b in range(B) for t in range(KT) for pr in range(2)]
        srow_parts = [(0, 1), (1, 4), (4, NT)]

        block = ctx.enter_context(nc.Block())

        @block.sync
        def _(sp):
            xv = x.rearrange("(c p) d -> p c d", p=P)
            sp.dma_start(x_sb[:, 0:CB, :], xv[:, 0:CB, :]).then_inc(x_in[0], 16)
            sp.dma_start(x_sb[:, CB:C, :], xv[:, CB:C, :]).then_inc(x_in[1], 16)
            sp.dma_start(wq_sb[:], w_qvo).then_inc(qo_in, 16)
            sp.dma_start(brow[:], rows_1.to_broadcast([P, 2 * D + E])).then_inc(brow_in, 16)
            sp.wait_ge(blank_ok, 2)
            for i in range(NT):
                sp.dma_start(slots_dram[i * P:(i + 1) * P, :], blank[:]).then_inc(blanked, 16)
            for e in range(E):
                sp.dma_start(w_sb[:, e, :], weights[e]).then_inc(w_in, 16)
            sp.dma_start(b2_sb[:, 0:E, :], b2.rearrange("e d -> (e d)").unsqueeze(0).to_broadcast([P, E * D])
                         .rearrange("p (e d) -> p e d", e=E)).then_inc(b2_in, 16)
            sp.wait_ge(owner_ok, 1)
            for i in range(NX):
                e = sp.value_load(owner[0:1, i:i + 1], min_val=0, max_val=E - 1)
                sp.dma_start(w_sb[:, E + i, :], weights[bass.ds(e, 1)].rearrange("e p n -> p (e n)")).then_inc(wx_in, 16)
                sp.dma_start(b2_sb[:, E + i, :], b2[bass.ds(e, 1)].to_broadcast([P, D])).then_inc(wx_in, 16)
            sp.wait_ge(sent, 16 * C)
            for i, (a, z) in enumerate(srow_parts):
                sp.dma_start(srow[:, a:z, :], slots_dram[a * P:z * P, :].rearrange("(n p) r -> p n r", p=P)
                             ).then_inc(srow_in[i], 16)

        @block.gpsimd
        def _(pool):
            gp = nc.gpsimd
            gp.memset(half[:], -0.5).then_inc(half_ok, 1)
            gp.memset(blank[:], 0.0).then_inc(blank_ok, 1)
            pool.wait_ge(blank_ok, 1)
            gp.memset(blank[:, TOK:TOK + 1].bitcast(I32), NTOK).then_inc(blank_ok, 1)
            gp.iota(rows[:, :, TOK:TOK + 1].bitcast(I32).rearrange("p c o -> p (c o)"), pattern=[[P, C]], base=0,
                    channel_multiplier=1).then_inc(tok_ok, 1)
            pool.wait_ge(kv_in, 48)
            gp.tensor_copy(wkrep[:], wk_sb[:].rearrange("p (g d) -> p g d", g=G).unsqueeze(2).to_broadcast([P, G, 4, GD])
                           ).then_inc(wkrep_ok, 1)
            for b in range(B):
                gp.tensor_copy(ctxrep[:, b, 0:HG * SK].rearrange("p (h k) -> p h k", h=HG),
                               ctx_sb[:, b, :].unsqueeze(1).to_broadcast([P, HG, SK])).then_inc(ctxrep_ok, 1)
            gp.memset(ctxrep[:, :, HG * SK:KC], 0.0).then_inc(ctxrep_ok, 1)

            for b in range(B):
                cs = slice(b * CB, (b + 1) * CB)
                pool.wait_ge(aggr_ok, b + 1)
                gp.tensor_scalar(var_eps[:, cs], ln1[:, cs, 1], EPS, None, ALU.add).then_inc(pool_step, 1)
                pool.wait_ge(pool_step, b + 1)
                if b == 0:
                    pool.wait_ge(half_ok, 1)
                gp.tensor_tensor(rstd1[:, cs], var_eps[:, cs], half[:, cs], ALU.pow).then_inc(rstd_ok, 1)
            gp.memset(kblk[:, :, :, HG * SK:KC].bitcast(F32), 0.0).then_inc(kblk_ok, 1)
            pool.wait_ge(brow_in, 16)
            pool.wait_ge(cst_in, 16)
            gp.tensor_tensor(bvm[:], cst[0:KR, VMASK:VMASK + KT * P].rearrange("p (t n) -> p t n", t=KT),
                             brow[0:KR, 0:D].unsqueeze(1).to_broadcast([KR, KT, P]), ALU.mult).then_inc(bvm_ok, 1)
            gp.tensor_copy(tri_bf[:], cst[:, UPPER:UPPER + 2 * P]).then_inc(tri_ok, 1)
            for b in range(B):
                cs = slice(b * CB, (b + 1) * CB)
                pool.wait_ge(xn_ok, C)
                gp.tensor_tensor(x_sb[:, cs, :], x_sb[:, cs, :], brow[:, D:2 * D].unsqueeze(1).to_broadcast([P, CB, D]),
                                 ALU.add).then_inc(xb_ok, 1)
            for b in range(B):
                cs = slice(b * CB, (b + 1) * CB)
                pool.wait_ge(aggr2_ok, b + 1)
                gp.tensor_scalar(var_eps[:, cs], rows[:, cs, RSTD], EPS, None, ALU.add).then_inc(pool_step, 1)
                pool.wait_ge(pool_step, B + b + 1)
                gp.tensor_tensor(rows[:, cs, RSTD], var_eps[:, cs], half[:, cs], ALU.pow).then_inc(rstd2_ok, 1)
            pool.wait_ge(blanked, 16 * NT)
            pool.wait_ge(slot_ok, 1)
            pool.wait_ge(prob_row_ok, 1)
            pool.wait_ge(tok_ok, 1)
            for c in range(C):
                gp.indirect_dma_start(slots_dram, bass.IndirectOffsetOnAxis(ap=slot[:, c:c + 1], axis=0),
                                      rows[:, c, :], None, bounds_check=NT * P - 1, oob_is_err=False).then_inc(sent, 16)
            for i in range(NT):
                pool.wait_ge(o_ok, i + 1)
                gp.indirect_dma_start(out, bass.IndirectOffsetOnAxis(ap=srow[:, i, TOK:TOK + 1].bitcast(I32), axis=0),
                                      o_sb[:, i, :], None, bounds_check=NTOK - 1, oob_is_err=False).then_inc(stored, 16)
            pool.wait_ge(stored, 16 * NT)

        @block.vector
        def _(dve):
            v = nc.vector
            steps = [0]

            def done(ins):
                steps[0] += 1
                ins.then_inc(dve_step, 1)
                dve.wait_ge(dve_step, steps[0])

            def moments(src, dst, ready):
                for c in range(src[0], src[1]):
                    ins = v.bn_stats(stats[:, c, :], src[2][:, c, 0:D])
                done(ins)
                for c in range(src[0], src[1]):
                    ins = v.bn_aggr(dst[:, c, :], stats[:, c, :])
                ins.then_inc(ready, 1)

            for b in range(B):
                dve.wait_ge(x_in[b], 16)
                moments((b * CB, (b + 1) * CB, x_sb), ln1, aggr_ok)
            dve.wait_ge(k_ok, 1)
            dve.wait_ge(cst_in, 16)
            done(v.tensor_tensor(kf[:].rearrange("p a (g k) -> p a g k", g=2),
                                 k_ps[:, :, 0:2 * B * SK].rearrange("p a (g k) -> p a g k", g=2),
                                 bk_sb[:, 0:G].rearrange("p (a g) -> p a g", a=2).unsqueeze(3).to_broadcast([P, 2, 2, B * SK]),
                                 ALU.add))
            kfg = kf[:].rearrange("p a (g k) -> p (a g) k", g=2)
            done(v.tensor_copy(kpart[:], kfg))
            for quad in (1, 3):
                qs = slice(quad * GD, (quad + 1) * GD)
                ins = v.tensor_tensor(kpart[qs], kfg[qs], kpart[qs].bitcast(F32), ALU.subtract)
            done(ins)
            kb = kpart[:].rearrange("p g (b k) -> p b g k", b=B).bitcast(F32)
            for h in range(HG):
                for b in range(B):
                    v.tensor_scalar(kblk[:, b, :, h * SK:(h + 1) * SK], kb[:, b], cst[:, KMASK + h:KMASK + h + 1], None,
                                    ALU.mult).then_inc(kblk_ok, 1)
            for b in range(B):
                dve.wait_ge(rstd_ok, b + 1)
                for c in range(b * CB, (b + 1) * CB):
                    v.tensor_scalar(xn[:, c, :], x_sb[:, c, :], ln1[:, c, 0:1], rstd1[:, c:c + 1],
                                    ALU.subtract, ALU.mult).then_inc(xn_ok, 1)
                if b == 0:
                    v.tensor_copy(sel[:], cst[:, SEL_HI:SEL_HI + 2 * G * P]).then_inc(sel_ok, 1)

            def split_low(b):
                dve.wait_ge(qhi_ok, b + 1)
                v.scalar_tensor_tensor(q_part[:, b, 1, :], q_ps[:], bk_sb[:, G:G + 1], q_part[:, b, 0, :].bitcast(F32),
                                       ALU.add, ALU.subtract).then_inc(qlo_ok, 1)

            def copy_stack(n):
                dve.wait_ge(stack_ok, n + 1)
                v.tensor_copy(q_stack[:, n // G, n % G, :], stack_ps[n % 2][:]).then_inc(stacked, 1)

            split_low(0)
            for n in range(G):
                copy_stack(n)
            dve.wait_ge(v_ok, 1)
            dve.wait_ge(bvm_ok, 1)
            for b in range(B):
                ins = v.tensor_tensor(vtmp[:, b, :], v_ps[0:KR, b, 0:KT * P], cst[0:KR, VMASK:VMASK + KT * P], ALU.mult)
                ins.then_inc(v_read, 1)
            dve.wait_ge(v_read, B)
            for b in range(B):
                v.tensor_tensor(vblk[:, b].rearrange("p t n -> p (t n)"), vtmp[:, b, :],
                                bvm[:].rearrange("p t n -> p (t n)"), ALU.add).then_inc(vblk_ok, 1)
            split_low(1)
            for n in range(G, 2 * G):
                copy_stack(n)
            for b in range(B):
                dve.wait_ge(att_ok, b + 1)
                v.tensor_copy(attT[:, b, :], att_ps[b][:]).then_inc(att_copied, 1)
                cs = slice(b * CB, (b + 1) * CB)
                dve.wait_ge(y_ok, b + 1)
                dve.wait_ge(xb_ok, b + 1)
                ins = v.tensor_tensor(rows[:, cs, 0:D], y_ps[b][:].rearrange("p (c d) -> p c d", c=CB), x_sb[:, cs, :], ALU.add)
                ins.then_inc(x1_ok, 1)
                dve.wait_ge(x1_ok, b + 1)
                moments((b * CB, (b + 1) * CB, rows), rows[:, :, MEAN:RSTD + 1], aggr2_ok)
                dve.wait_ge(rstd2_ok, b + 1)
                for c in range(b * CB, (b + 1) * CB):
                    v.tensor_scalar(xn[:, c, :], rows[:, c, 0:D], rows[:, c, MEAN:MEAN + 1], rows[:, c, RSTD:RSTD + 1],
                                    ALU.subtract, ALU.mult).then_inc(xn2_ok, 1)
                dve.wait_ge(x2T_ok, b + 1)
                v.tensor_copy(xn2T[:, b, :], x2T_ps[b][:]).then_inc(x2T_copied, 1)
                dve.wait_ge(logit_ok, b + 1)
                v.tensor_tensor(logit[:, cs, :], logit_ps[b][:, 0:CB * E].rearrange("p (c e) -> p c e", c=CB),
                                brow[:, 2 * D:2 * D + E].unsqueeze(1).to_broadcast([P, CB, E]), ALU.add).then_inc(logit_read, 1)
            dve.wait_ge(logit_read, B)
            bc = [P, C, E]
            done(v.tensor_reduce(lmax[:], logit[:], AX, ALU.max))
            v.tensor_tensor(lsub[:], logit[:], lmax[:].unsqueeze(2).to_broadcast(bc), ALU.subtract).then_inc(lsub_ok, 1)
            done(v.tensor_tensor(eq[:], logit[:], lmax[:].unsqueeze(2).to_broadcast(bc), ALU.is_equal))
            done(v.tensor_tensor(eq[:], eq[:], cst[:, DESC:DESC + E].unsqueeze(1).to_broadcast(bc), ALU.mult))
            done(v.tensor_reduce(first[:], eq[:], AX, ALU.max))
            v.tensor_tensor(chosen[:], eq[:], first[:].unsqueeze(2).to_broadcast(bc), ALU.is_equal).then_inc(chosen_ok, 1)
            dve.wait_ge(lexp_ok, 1)
            done(v.tensor_reduce(lsum[:], lexp[:], AX, ALU.add))
            v.reciprocal(rows[:, :, PROB], lsum[:]).then_inc(prob_row_ok, 1)
            dve.wait_ge(rank_ok, 1)
            done(v.tensor_tensor(over[:], count_ps.unsqueeze(2).to_broadcast([P, E, NX]),
                                 cst[:, THRESH:THRESH + NX].unsqueeze(1).to_broadcast([P, E, NX]), ALU.is_gt))
            done(v.tensor_reduce(extra[:], over[:], AX, ALU.add))
            done(v.tensor_tensor(before[:], extra[:].unsqueeze(1).to_broadcast([P, E, E]),
                                 cst[:, TRI:TRI + E * E].rearrange("p (e f) -> p e f", e=E), ALU.mult))
            done(v.tensor_reduce(opened[:], before[:], AX, ALU.add))
            done(v.scalar_tensor_tensor(jump[:], opened[:], float(P), cst[:, JUMP:JUMP + E], ALU.mult, ALU.add))
            rk = rank_ps.rearrange("p (c e) -> p c e", c=C)
            done(v.scalar_tensor_tensor(slot8[:], rk, P - 0.5, jump[:].unsqueeze(1).to_broadcast(bc), ALU.is_gt, ALU.mult))
            done(v.tensor_tensor(slot8[:], rk, slot8[:], ALU.add))
            done(v.tensor_tensor(slot8[:], slot8[:], cst[:, BASE:BASE + E].unsqueeze(1).to_broadcast(bc), ALU.add))
            done(v.tensor_tensor(slot8[:], slot8[:], chosen[:], ALU.mult))
            done(v.tensor_reduce(lmax[:], slot8[:], AX, ALU.add))
            v.tensor_copy(slot[:], lmax[:]).then_inc(slot_ok, 1)
            done(v.tensor_tensor(upto[:], opened[0:1, :], extra[0:1, :], ALU.add))
            done(v.tensor_tensor(cmp_t[:], upto[:].unsqueeze(1).to_broadcast([1, NX, E]),
                                 cst[0:1, TILE_NO:TILE_NO + NX].unsqueeze(2).to_broadcast([1, NX, E]), ALU.is_le))
            done(v.tensor_reduce(owner_f[:], cmp_t[:], AX, ALU.add))
            v.tensor_scalar(owner[:], owner_f[:], float(E - 1), None, ALU.min).then_inc(owner_ok, 1)

            def normalise(i):
                for n, (a, z) in enumerate(srow_parts):
                    if i == a:
                        dve.wait_ge(srow_in[n], 16)
                v.tensor_scalar(sxn[:, i, :], srow[:, i, 0:D], srow[:, i, MEAN:MEAN + 1], srow[:, i, RSTD:RSTD + 1],
                                ALU.subtract, ALU.mult).then_inc(sxn_ok, 1)

            def copy_T(i):
                dve.wait_ge(sT_ok, i + 1)
                v.tensor_copy(sxnT[:, i, :], t_ps[i % 2][:, 0:P]).then_inc(sT_copied, 1)

            def finish(i):
                dve.wait_ge(f_ok, i + 1)
                if i == 0:
                    dve.wait_ge(b2_in, 16)
                if i == E:
                    dve.wait_ge(wx_in, 32 * NX)
                v.tensor_tensor(y_sb[:, i, :], f_ps[i % 2][:, 0:D], b2_sb[:, i, :], ALU.add).then_inc(f_read, 1)
                dve.wait_ge(f_read, i + 1)
                v.scalar_tensor_tensor(o_sb[:, i, :], y_sb[:, i, :], srow[:, i, PROB:PROB + 1], srow[:, i, 0:D],
                                       ALU.mult, ALU.add).then_inc(o_ok, 1)

            normalise(0)
            copy_T(0)
            normalise(1)
            for i in range(NT):
                if i + 2 < NT:
                    normalise(i + 2)
                if i + 1 < NT:
                    copy_T(i + 1)
                finish(i)

        @block.scalar
        def _(act):
            a = nc.scalar
            act.dma_start(ctx_sb[:], ctx_t).then_inc(kv_in, 16)
            act.dma_start(wk_sb[:], wk4).then_inc(kv_in, 16)
            act.dma_start(bk_sb[:], bk4).then_inc(kv_in, 16)
            act.dma_start(cst[:], const).then_inc(cst_in, 16)

            def copy_xT(b):
                act.wait_ge(xT_ok, b + 1)
                a.copy(xnT[:, b, :], xT_ps[b][:]).then_inc(xT_copied, 1)

            def split_high(b):
                act.wait_ge(q_ok, b + 1)
                if b == 0:
                    act.wait_ge(kv_in, 48)
                a.activation(q_part[:, b, 0, :], q_ps[:], ACT.Identity, bias=bk_sb[:, G:G + 1]).then_inc(qhi_ok, 1)

            def sigmoid(n):
                b, t, pr = units[n]
                act.wait_ge(score_ok, n + 1)
                a.activation(probs[:, b, t, 2 * pr:2 * pr + 2, :], pair[n % 2][0:KR, :, :], ACT.Sigmoid,
                             scale=float(DH) ** -0.5).then_inc(prob_ok, 1)

            copy_xT(0)
            split_high(0)
            for n in range(len(units)):
                if n == 1:
                    copy_xT(1)
                if n == 2:
                    split_high(1)
                sigmoid(n)
            act.wait_ge(lsub_ok, 1)
            a.activation(lexp[:], lsub[:], ACT.Exp).then_inc(lexp_ok, 1)
            for i in range(NT):
                act.wait_ge(h_ok, i + 1)
                if i >= 3:
                    act.wait_ge(f_ok, i - 2)
                if i == E:
                    act.wait_ge(wx_in, 32 * NX)
                for k in range(FC):
                    a.activation(hT[:, i % 3, k * P:(k + 1) * P], h_ps[i % 2][:, k * P:(k + 1) * P], ACT.Gelu_apprx_tanh,
                                 bias=w_sb[:, i, WB + k:WB + k + 1]).then_inc(gelu_ok, 1)

        @block.tensor
        def _(pe):
            mm, tr = nc.tensor.matmul, nc.tensor.transpose
            ident = cst[:, IDENT:IDENT + P]

            def transpose_x(b):
                for c in range(CB):
                    pe.wait_ge(xn_ok, b * CB + c + 1)
                    ins = tr(xT_ps[b][:, c * P:(c + 1) * P], xn[:, b * CB + c, :], ident)
                ins.then_inc(xT_ok, 1)

            def project_q(b):
                pe.wait_ge(xT_copied, b + 1)
                if b:
                    pe.wait_ge(qlo_ok, b)
                mm(q_ps[:], wq_sb[:, 0:D], xnT[:, b, :], start=True, stop=True).then_inc(q_ok, 1)

            def stack_q(n):
                b, g = n // G, n % G
                if g == 0:
                    pe.wait_ge(qlo_ok, b + 1)
                if n == 0:
                    pe.wait_ge(sel_ok, 1)
                if n >= 2:
                    pe.wait_ge(stacked, n - 1)
                mm(stack_ps[n % 2][:], sel[:, g * P:(g + 1) * P], q_part[:, b, 0, :], start=True, stop=False)
                mm(stack_ps[n % 2][:], sel[:, (G + g) * P:(G + g + 1) * P], q_part[:, b, 1, :], start=False,
                   stop=True).then_inc(stack_ok, 1)

            def score(n):
                b, t, pr = units[n]
                if n == 0:
                    pe.wait_ge(kblk_ok, 1 + HG * B)
                if n == 1:
                    pe.wait_ge(v_read, B)
                if n >= 2:
                    pe.wait_ge(prob_ok, n - 1)
                for j in range(2):
                    g = 2 * pr + j
                    if t == 0:
                        pe.wait_ge(stacked, b * G + g + 1)
                    ins = mm(pair[n % 2][0:KR, j, :], kblk[:, b, g, t * KR:(t + 1) * KR], q_stack[:, b, g, :],
                             start=True, stop=True)
                ins.then_inc(score_ok, 1)

            def attend(b, t):
                pe.wait_ge(prob_ok, 2 * (b * KT + t + 1))
                if t == 0:
                    pe.wait_ge(vblk_ok, B)
                    pe.wait_ge([xT_copied, qlo_ok][b], B)
                for g in range(G):
                    ins = mm(att_ps[b][g * GD:(g + 1) * GD, :], vblk[:, b, t, g * GD:(g + 1) * GD],
                             probs[:, b, t, g, :], start=(t == 0), stop=(t == KT - 1))
                if t == KT - 1:
                    ins.then_inc(att_ok, 1)

            def project_out(b):
                pe.wait_ge(att_copied, b + 1)
                pe.wait_ge(stacked, 2 * G)
                if b:
                    pe.wait_ge(logit_read, 0 + b)
                for c in range(CB):
                    ins = mm(y_ps[b][:, c * D:(c + 1) * D], attT[:, b, c * P:(c + 1) * P], wq_sb[:, 2 * D:3 * D],
                             start=True, stop=True)
                ins.then_inc(y_ok, 1)

            def transpose_x2(b):
                for c in range(CB):
                    pe.wait_ge(xn2_ok, b * CB + c + 1)
                    ins = tr(x2T_ps[b][:, c * P:(c + 1) * P], xn[:, b * CB + c, :], ident)
                ins.then_inc(x2T_ok, 1)

            def router(b):
                pe.wait_ge(x2T_copied, b + 1)
                pe.wait_ge(x1_ok, b + 1)
                for c in range(CB):
                    ins = mm(logit_ps[b][:, c * E:(c + 1) * E], xn2T[:, b, c * P:(c + 1) * P], wq_sb[:, 3 * D:3 * D + E],
                             start=True, stop=True)
                ins.then_inc(logit_ok, 1)

            pe.wait_ge(kv_in, 48)
            pe.wait_ge(wkrep_ok, 1)
            for g in range(G):
                ins = mm(k_ps[:, g // 2, (g % 2) * B * SK:(g % 2 + 1) * B * SK], wkrep[:, g].rearrange("p r d -> p (r d)"),
                         ctx_sb[:].rearrange("p b k -> p (b k)"), start=True, stop=True)
            ins.then_inc(k_ok, 1)
            pe.wait_ge(ctxrep_ok, B + 1)
            pe.wait_ge(qo_in, 16)
            for b in range(B):
                for t in range(KT):
                    ins = mm(v_ps[0:KR, b, t * P:(t + 1) * P], ctxrep[:, b, t * KR:(t + 1) * KR], wq_sb[:, D:2 * D],
                             start=True, stop=True)
            ins.then_inc(v_ok, 1)
            pe.wait_ge(cst_in, 16)
            transpose_x(0)
            project_q(0)
            transpose_x(1)
            stack_q(0)
            stack_q(1)
            score(0)
            stack_q(2)
            stack_q(3)
            score(1)
            project_q(1)
            score(2)
            attend(0, 0)
            stack_q(4)
            stack_q(5)
            score(3)
            stack_q(6)
            stack_q(7)
            score(4)
            attend(0, 1)
            score(5)
            score(6)
            attend(0, 2)
            score(7)
            project_out(0)
            score(8)
            attend(1, 0)
            score(9)
            transpose_x2(0)
            score(10)
            attend(1, 1)
            router(0)
            score(11)
            attend(1, 2)
            project_out(1)
            transpose_x2(1)
            router(1)
            pe.wait_ge(chosen_ok, 1)
            pe.wait_ge(tri_ok, 1)
            pe.wait_ge(prob_ok, len(units))
            ch = chosen[:].rearrange("p c e -> p (c e)")
            mm(rank_ps, tri_bf[:, 0:P], ch, start=True, stop=False, skip_group_check=True)
            for s in range(1, C):
                mm(pair[0][:, 0, s * E:C * E], tri_bf[:, P:2 * P], ch[:, 0:(C - s) * E], start=False, stop=(s == C - 1),
                   skip_group_check=True)
            for c in range(C):
                ins = mm(count_ps, tri_bf[:, P:2 * P], ch[:, c * E:(c + 1) * E], start=False, stop=(c == C - 1),
                         skip_group_check=True)
            ins.then_inc(rank_ok, 1)

            def transpose_slots(i):
                pe.wait_ge(sxn_ok, i + 1)
                if i >= 2:
                    pe.wait_ge(sT_copied, i - 1)
                tr(t_ps[i % 2][:, 0:P], sxn[:, i, :], ident).then_inc(sT_ok, 1)

            def up(i):
                pe.wait_ge(sT_copied, i + 1)
                if i == 0:
                    pe.wait_ge(w_in, 16 * E)
                if i == E:
                    pe.wait_ge(wx_in, 32 * NX)
                if i >= 2:
                    pe.wait_ge(gelu_ok, FC * (i - 1))
                for k in range(FC):
                    ins = mm(h_ps[i % 2][:, k * P:(k + 1) * P], w_sb[:, i, W1 + k * P:W1 + (k + 1) * P], sxnT[:, i, :],
                             start=True, stop=True)
                ins.then_inc(h_ok, 1)

            def down(i):
                if i >= 2:
                    pe.wait_ge(f_read, i - 1)
                for k in range(FC):
                    pe.wait_ge(gelu_ok, FC * i + k + 1)
                    ins = mm(f_ps[i % 2][:, 0:D], hT[:, i % 3, k * P:(k + 1) * P], w_sb[:, i, W2 + k * D:W2 + (k + 1) * D],
                             start=(k == 0), stop=(k == FC - 1))
                ins.then_inc(f_ok, 1)

            transpose_slots(0)
            for i in range(NT):
                if i + 1 < NT:
                    transpose_slots(i + 1)
                up(i)
                if i >= 1:
                    down(i - 1)
            down(NT - 1)


def kernel(x, ctx_1024, L0_xattn_Wq, L0_xattn_bq, L0_xattn_Wk, L0_xattn_bk, L0_xattn_Wv, L0_xattn_bv, L0_xattn_Wo,
           L0_xattn_bo, L0_ffn_switch_w, L0_ffn_switch_b, L0_ffn_w1, L0_ffn_b1, L0_ffn_w2, L0_ffn_b2):
    import concourse.bacc as bacc
    from concourse.bass_utils import run_bass_kernel_spmd

    a = np.asarray
    cat = np.concatenate
    w1, w2, b1 = a(L0_ffn_w1), a(L0_ffn_w2), a(L0_ffn_b1)
    arrays = {
        "tokens": a(x).reshape(NTOK, D),
        "wkT": a(L0_xattn_Wk).T,
        "ctxT": a(ctx_1024).reshape(B * SK, D).T.reshape(D, B, SK),
        "bias_kq": cat([np.tile(a(L0_xattn_bk).reshape(G, 1, GD), (1, 4, 1)).reshape(G, P).T,
                        a(L0_xattn_bq).reshape(D, 1)], axis=1),
        "w_qvo": cat([a(L0_xattn_Wq).T, a(L0_xattn_Wv).T, a(L0_xattn_Wo).T, a(L0_ffn_switch_w)], axis=1),
        "bias_row": cat([a(L0_xattn_bv), a(L0_xattn_bo), a(L0_ffn_switch_b)]).reshape(1, 2 * D + E),
        "const": constants(),
        "weights": cat([w1, w2.reshape(E, FC, P, D).transpose(0, 2, 1, 3).reshape(E, P, F),
                        b1.reshape(E, FC, P).transpose(0, 2, 1)], axis=2),
        "b2": a(L0_ffn_b2),
    }
    arrays = {k: np.ascontiguousarray(v) for k, v in arrays.items()}
    nc = bacc.Bacc("TRN2", target_bir_lowering=False, num_devices=1)
    aps = [nc.dram_tensor(k, v.shape, mybir.dt.from_np(v.dtype), kind="ExternalInput").ap() for k, v in arrays.items()]
    out = nc.dram_tensor("result", (NTOK, D), mybir.dt.float32, kind="ExternalOutput").ap()
    build_program(nc, *aps, out)
    r = run_bass_kernel_spmd(nc, [arrays], core_ids=[0])
    return r.results[0]["result"].reshape(B, S, D)
```

```python
from contextlib import ExitStack

import numpy as np

import concourse.bass as bass
from concourse import mybir

P = 128
B, S, D = 2, 512, 128
SK = 77
H, DH = 16, 8
E, F = 8, 512
NTOK = B * S
C = NTOK // P
CB = S // P
G = 4
GD = D // G
HG = H // G
KT = 3
KR = -(-HG * SK // KT)
KC = KT * KR
FC = F // P
NX = C - 1
NT = E + NX
W1, W2 = 0, F
WB = 2 * F
WCOLS = 2 * F + FC
MEAN, RSTD, PROB, TOK = D, D + 1, D + 2, D + 3
ROW = D + 4
EPS = 1e-5
AHEAD = 3
LEAD = 2

KW, KB, QB, IDENT = 0, D, D + G, D + G + 1
KMASK = IDENT + P
KSIGN = KMASK + HG
CTX = KSIGN + 1
NFIRST = CTX + B * SK
QW, VW, OW, RW = 0, D, 2 * D, 3 * D
NSECOND = 3 * D + E
VMASK = 0
DESC = VMASK + KT * P
TRI = DESC + E
THRESH = TRI + E * E
JUMP = THRESH + NX
BASE = JUMP + E
TILE_NO = BASE + E
NCONST = TILE_NO + NX


def first_constants():
    p = np.arange(P)
    t = np.zeros((P, P + HG + 1), np.float32)
    t[:, 0:P] = np.eye(P)
    for h in range(HG):
        t[:, P + h] = (p % GD) // DH == h
    t[:, P + HG] = -((p // GD) % 2)
    return t


def constants():
    t = np.zeros((P, NCONST), np.float32)
    p = np.arange(P)
    for k in range(KT):
        for r in range(KR):
            key = k * KR + r
            if key < HG * SK:
                t[r, VMASK + k * P:VMASK + (k + 1) * P] = (p % GD) // DH == key // SK
    e = np.arange(E)
    t[:, DESC:DESC + E] = E - e
    t[:, TRI:TRI + E * E] = (e[None, :] < e[:, None]).reshape(-1)
    t[:, THRESH:THRESH + NX] = P * (1 + np.arange(NX))
    t[:, JUMP:JUMP + E] = (E - 1) * P - P * e
    t[:, BASE:BASE + E] = P * e
    t[:, TILE_NO:TILE_NO + NX] = np.arange(NX)
    return t


def build_program(nc, x, w_first, w_second, rows_1, const, weights, b2, out):
    F32, F32R, BF16, I32 = mybir.dt.float32, mybir.dt.float32r, mybir.dt.bfloat16, mybir.dt.int32
    ALU, ACT, AX = mybir.AluOpType, mybir.ActivationFunctionType, mybir.AxisListType.X
    ctx = ExitStack()
    with ctx:
        def sb(name, shape, dt=F32):
            return ctx.enter_context(nc.sbuf_tensor(name, shape, dt))

        def sem(name):
            return ctx.enter_context(nc.semaphore(name))

        x_sb = sb("x_sb", [P, C, D])
        w1st = sb("w1st", [P, NFIRST])
        w2nd = sb("w2nd", [P, NSECOND])
        cst = sb("cst", [P, NCONST])
        brow = sb("brow", [P, 2 * D + E])
        wkrep = sb("wkrep", [P, G, 4, GD])
        ctxrep = sb("ctxrep", [P, B, KC])
        bvm = sb("bvm", [KR, KT, P])
        sel = sb("sel", [P, 2, G, 4, GD], F32R)
        tri_bf = sb("tri_bf", [P, 2 * P], BF16)
        mean_w = sb("mean_w", [P, P])
        rw_c = sb("rw_c", [P, E])
        half = sb("half", [P, C])
        warm = sb("warm", [P, 2])
        stats = sb("stats", [P, C, 6])
        ln1 = sb("ln1", [P, C, 2])
        var_eps = sb("var_eps", [P, C])
        rstd1 = sb("rstd1", [P, C])
        xn = sb("xn", [P, C, D])
        xnT = sb("xnT", [P, B, S])
        q_part = sb("q_part", [P, B, 2, S], F32R)
        q_stack = sb("q_stack", [P, B, G, S], F32R)
        kf = sb("kf", [P, G, B * SK])
        kpart = sb("kpart", [P, G, B * SK], F32R)
        kblk = sb("kblk", [P, B, G, KC], F32R)
        vtmp = sb("vtmp", [KR, B, KT * P])
        vblk = sb("vblk", [KR, B, KT, P])
        attT = sb("attT", [P, B, S])
        rows = sb("rows", [P, C, ROW])
        logit = sb("logit", [P, C, E])
        lmax = sb("lmax", [P, C])
        lsub = sb("lsub", [P, C, E])
        sig = sb("sig", [P, 2, C, E])
        lexp = sb("lexp", [P, C, E])
        lsum = sb("lsum", [P, C])
        eq = sb("eq", [P, C, E])
        first = sb("first", [P, C])
        chosen = sb("chosen", [P, C, E], BF16)
        over = sb("over", [P, E, NX])
        extra = sb("extra", [P, B, E])
        before = sb("before", [P, E, E])
        opened = sb("opened", [P, B, E])
        total = sb("total", [P, 1])
        jump = sb("jump", [P, B, E])
        thresh1 = sb("thresh1", [P, E])
        slot8 = sb("slot8", [P, C, E])
        late = sb("late", [P, CB, E])
        slotf = sb("slotf", [P, C])
        slot = sb("slot", [P, C], I32)
        upto = sb("upto", [1, B, E])
        cmp_t = sb("cmp_t", [1, B, NX, E])
        owner_f = sb("owner_f", [1, B, NX])
        owner_s = sb("owner_s", [1, NX])
        owner = sb("owner", [1, NX], I32)
        blank = sb("blank", [P, ROW])
        shared = sb("shared", [P, B * KT * G * S])
        probs = shared[0:KR, :].rearrange("p (b t g s) -> p b t g s", b=B, t=KT, g=G)
        srow, sxn, sxnT, y_sb, o_sb = (
            shared[:, NT * at:NT * (at + n)].rearrange("p (i n) -> p i n", i=NT)
            for at, n in ((0, ROW), (ROW, D), (ROW + D, P), (ROW + D + P, D), (ROW + 2 * D + P, D)))
        hT = shared[:, NT * (ROW + 3 * D + P):NT * (ROW + 3 * D + P) + 3 * F].rearrange("p (i n) -> p i n", i=3)
        w_sb = sb("w_sb", [P, NT, WCOLS])
        b2_sb = sb("b2_sb", [P, NT, D])

        pair = [ctx.enter_context(nc.psum_tensor(f"pair{i}", [P, 2, 512], F32)) for i in range(2)]
        bank = [ctx.enter_context(nc.psum_tensor(f"bank{i}", [P, 512], F32)) for i in range(4)]
        k_ps, v_ps = pair
        xT_ps = [bank[0], bank[1]]
        q_ps = bank[2]
        stack_ps = [bank[0], bank[3]]
        att_ps = [bank[1], bank[2]]
        y_ps = [[bank[0][:, c * D:(c + 1) * D] for c in range(CB)],
                [t[:, 0:D] for t in (bank[0], bank[3], bank[1], pair[0][:, 0, :])]]
        x1T_ps = [[bank[3][:, c * P:(c + 1) * P] for c in range(CB)],
                  [t[:, 0:P] for t in (pair[0][:, 1, :], pair[1][:, 0, :], pair[1][:, 1, :], bank[0])]]
        logit_ps = [bank[1], bank[3]]
        rank_bank = [bank[0], bank[1]]
        rank_ps = [t[:, 0:CB * E].rearrange("p (c e) -> p c e", c=CB) for t in rank_bank]
        count_ps = [t[:, CB * E:CB * E + E] for t in rank_bank]
        mean_ps = pair[1][:, 1, KT * P:KT * P + E]
        h_ps = [pair[1][:, 0, :], pair[1][:, 1, :]]
        t_ps = [bank[0], bank[1]]
        f_ps = [bank[2], bank[3]]

        slots_dram = nc.dram_tensor("slots_dram", (NT * P, ROW), F32).ap()

        x_in = [sem(f"x_in{b}") for b in range(B)]
        first_in, second_in, cst_in, brow_in = sem("first_in"), sem("second_in"), sem("cst_in"), sem("brow_in")
        w_in, wx_in, b2_in = sem("w_in"), sem("wx_in"), sem("b2_in")
        blank_ok, blanked, sent, stored = sem("blank_ok"), sem("blanked"), sem("sent"), sem("stored")
        srow_in = [sem(f"srow_in{i}") for i in range(3)]
        pool_step, dve_step = sem("pool_step"), sem("dve_step")
        half_ok, ones_ok, sel_zero, tok_ok = sem("half_ok"), sem("ones_ok"), sem("sel_zero"), sem("tok_ok")
        wkrep_ok, ctxrep_ok, bvm_ok, tri_ok, sel_ok = (sem("wkrep_ok"), sem("ctxrep_ok"), sem("bvm_ok"),
                                                       sem("tri_ok"), sem("sel_ok"))
        rw_ok = sem("rw_ok")
        aggr_ok, rstd_ok, xn_ok, xT_ok, xT_copied = (sem("aggr_ok"), sem("rstd_ok"), sem("xn_ok"),
                                                     sem("xT_ok"), sem("xT_copied"))
        xb_ok = sem("xb_ok")
        k_ok, kpart_ok, kblk_ok, v_ok, v_read, vblk_ok = (sem("k_ok"), sem("kpart_ok"), sem("kblk_ok"),
                                                          sem("v_ok"), sem("v_read"), sem("vblk_ok"))
        q_ok, qhi_ok, qlo_ok, stack_ok = sem("q_ok"), sem("qhi_ok"), sem("qlo_ok"), sem("stack_ok")
        stacked = [sem(f"stacked{i}") for i in range(2)]
        score_ok, prob_ok, att_ok, att_copied = sem("score_ok"), sem("prob_ok"), sem("att_ok"), sem("att_copied")
        y_ok, x1_ok, aggr2_ok, rstd2_ok = sem("y_ok"), sem("x1_ok"), sem("aggr2_ok"), sem("rstd2_ok")
        x1T_ok, x1T_copied, logit_ok, logit_read = sem("x1T_ok"), sem("x1T_copied"), sem("logit_ok"), sem("logit_read")
        lsub_ok, sig_ok, chosen_ok, rank_ok, rank_read = (sem("lsub_ok"), sem("sig_ok"), sem("chosen_ok"),
                                                          sem("rank_ok"), sem("rank_read"))
        slot_ok, owner_ok, prob_row_ok = sem("slot_ok"), sem("owner_ok"), sem("prob_row_ok")
        sxn_ok, sT_ok, sT_copied, h_ok, gelu_ok, f_ok, f_read, o_ok = (
            sem("sxn_ok"), sem("sT_ok"), sem("sT_copied"), sem("h_ok"), sem("gelu_ok"), sem("f_ok"),
            sem("f_read"), sem("o_ok"))

        units = [(0, t, pr) for pr in range(2) for t in range(KT)] + [(1, t, pr) for t in range(KT) for pr in range(2)]
        ATT_AFTER = {(b, t): 1 + max(n for n, u in enumerate(units) if u[:2] == (b, t)) for b in range(B) for t in range(KT)}
        ACT_STACKS = (0, 2)
        srow_parts = [(0, 1), (1, 4), (4, NT)]

        block = ctx.enter_context(nc.Block())

        @block.sync
        def _(sp):
            xv = x.rearrange("(c p) d -> p c d", p=P)
            sp.dma_start(x_sb[:, 0:CB, :], xv[:, 0:CB, :]).then_inc(x_in[0], 16)
            sp.dma_start(w2nd[:], w_second).then_inc(second_in, 16)
            sp.dma_start(x_sb[:, CB:C, :], xv[:, CB:C, :]).then_inc(x_in[1], 16)
            sp.dma_start(cst[:], const).then_inc(cst_in, 16)
            sp.dma_start(brow[:], rows_1.to_broadcast([P, 2 * D + E])).then_inc(brow_in, 16)
            sp.wait_ge(blank_ok, 2)
            sp.dma_start(slots_dram.rearrange("(n p) r -> p n r", p=P), blank[:].unsqueeze(1).to_broadcast([P, NT, ROW])
                         ).then_inc(blanked, 16)
            for e in range(0, E, 2):
                sp.dma_start(w_sb[:, e:e + 2, :], weights[e:e + 2].rearrange("e p n -> p e n")).then_inc(w_in, 16)
            sp.dma_start(b2_sb[:, 0:E, :], b2.rearrange("e d -> (e d)").unsqueeze(0).to_broadcast([P, E * D])
                         .rearrange("p (e d) -> p e d", e=E)).then_inc(b2_in, 16)
            sp.wait_ge(sent, 16 * C)
            for i, (a, z) in enumerate(srow_parts):
                sp.dma_start(srow[:, a:z, :], slots_dram[a * P:z * P, :].rearrange("(n p) r -> p n r", p=P)
                             ).then_inc(srow_in[i], 16)
            sp.wait_ge(owner_ok, 1)
            for i in range(NX):
                e = sp.value_load(owner[0:1, i:i + 1], min_val=0, max_val=E - 1)
                sp.dma_start(w_sb[:, E + i, :], weights[bass.ds(e, 1)].rearrange("e p n -> p (e n)")).then_inc(wx_in, 16)
                sp.dma_start(b2_sb[:, E + i, :], b2[bass.ds(e, 1)].to_broadcast([P, D])).then_inc(wx_in, 16)

        @block.gpsimd
        def _(pool):
            gp = nc.gpsimd
            gp.memset(half[:], -0.5).then_inc(half_ok, 1)
            gp.memset(ctxrep[:, :, HG * SK:KC], 0.0).then_inc(ctxrep_ok, 1)
            gp.memset(sel[:].bitcast(F32), 0.0).then_inc(sel_zero, 1)
            gp.memset(blank[:], 0.0).then_inc(blank_ok, 1)
            pool.wait_ge(blank_ok, 1)
            gp.memset(blank[:, TOK:TOK + 1].bitcast(I32), NTOK).then_inc(blank_ok, 1)
            gp.iota(rows[:, :, TOK:TOK + 1].bitcast(I32).rearrange("p c o -> p (c o)"), pattern=[[P, C]], base=0,
                    channel_multiplier=1).then_inc(tok_ok, 1)
            gp.memset(mean_w[:], 1.0 / D).then_inc(ones_ok, 1)
            gp.memset(kblk[:, :, :, HG * SK:KC].bitcast(F32), 0.0).then_inc(kblk_ok, 1)
            gp.memset(tri_bf[:], 1.0).then_inc(tri_ok, 1)

            for b in range(B):
                cs = slice(b * CB, (b + 1) * CB)
                pool.wait_ge(aggr_ok, b + 1)
                gp.tensor_scalar(var_eps[:, cs], ln1[:, cs, 1], EPS, None, ALU.add).then_inc(pool_step, 1)
                pool.wait_ge(pool_step, b + 1)
                if b == 0:
                    pool.wait_ge(half_ok, 1)
                gp.tensor_tensor(rstd1[:, cs], var_eps[:, cs], half[:, cs], ALU.pow).then_inc(rstd_ok, 1)
            pool.wait_ge(tri_ok, 1)
            gp.affine_select(out=tri_bf[:, 0:P], in_=tri_bf[:, 0:P], compare_op=ALU.is_gt, fill=0.0, base=0,
                             pattern=[[1, P]], channel_multiplier=-1).then_inc(tri_ok, 1)
            pool.wait_ge(brow_in, 16)
            pool.wait_ge(cst_in, 16)
            gp.tensor_tensor(bvm[:], cst[0:KR, VMASK:VMASK + KT * P].rearrange("p (t n) -> p t n", t=KT),
                             brow[0:KR, 0:D].unsqueeze(1).to_broadcast([KR, KT, P]), ALU.mult).then_inc(bvm_ok, 1)
            for b in range(B):
                cs = slice(b * CB, (b + 1) * CB)
                pool.wait_ge(xn_ok, (b + 1) * CB)
                gp.tensor_tensor(x_sb[:, cs, :], x_sb[:, cs, :], brow[:, D:2 * D].unsqueeze(1).to_broadcast([P, CB, D]),
                                 ALU.add).then_inc(xb_ok, 1)
            for b in range(B):
                cs = slice(b * CB, (b + 1) * CB)
                pool.wait_ge(aggr2_ok, b + 1)
                gp.tensor_scalar(var_eps[:, cs], rows[:, cs, RSTD], EPS, None, ALU.add).then_inc(pool_step, 1)
                pool.wait_ge(pool_step, B + b + 1)
                gp.tensor_tensor(rows[:, cs, RSTD], var_eps[:, cs], half[:, cs], ALU.pow).then_inc(rstd2_ok, 1)
                if b == 0:
                    pool.wait_ge(blanked, 16)
                    pool.wait_ge(tok_ok, 1)
                pool.wait_ge(slot_ok, b + 1)
                pool.wait_ge(prob_row_ok, b + 1)
                for c in range(b * CB, (b + 1) * CB):
                    gp.indirect_dma_start(slots_dram, bass.IndirectOffsetOnAxis(ap=slot[:, c:c + 1], axis=0),
                                          rows[:, c, :], None, bounds_check=NT * P - 1, oob_is_err=False).then_inc(sent, 16)
            for i in range(NT):
                pool.wait_ge(o_ok, i + 1)
                gp.indirect_dma_start(out, bass.IndirectOffsetOnAxis(ap=srow[:, i, TOK:TOK + 1].bitcast(I32), axis=0),
                                      o_sb[:, i, :], None, bounds_check=NTOK - 1, oob_is_err=False).then_inc(stored, 16)
            pool.wait_ge(stored, 16 * NT)

        @block.vector
        def _(dve):
            v = nc.vector
            steps = [0]

            def done(ins):
                steps[0] += 1
                ins.then_inc(dve_step, 1)
                dve.wait_ge(dve_step, steps[0])

            def normalise_first(b):
                dve.wait_ge(rstd_ok, b + 1)
                for c in range(b * CB, (b + 1) * CB):
                    v.tensor_scalar(xn[:, c, :], x_sb[:, c, :], ln1[:, c, 0:1], rstd1[:, c:c + 1],
                                    ALU.subtract, ALU.mult).then_inc(xn_ok, 1)

            def moments(b):
                dve.wait_ge(x_in[b], 16)
                for c in range(b * CB, (b + 1) * CB):
                    ins = v.bn_stats(stats[:, c, :], x_sb[:, c, :])
                done(ins)
                for c in range(b * CB, (b + 1) * CB):
                    ins = v.bn_aggr(ln1[:, c, :], stats[:, c, :])
                ins.then_inc(aggr_ok, 1)

            def split_low(b):
                dve.wait_ge(qhi_ok, b + 1)
                v.scalar_tensor_tensor(q_part[:, b, 1, :], q_ps[:], w1st[:, QB:QB + 1], q_part[:, b, 0, :].bitcast(F32),
                                       ALU.add, ALU.subtract).then_inc(qlo_ok, 1)

            def copy_stack(n):
                dve.wait_ge(stack_ok, n + 1)
                v.tensor_copy(q_stack[:, n // G, n % G, :], stack_ps[n % 2][:]).then_inc(stacked[n % 2], 1)

            moments(0)
            dve.wait_ge(first_in, 16)
            dve.wait_ge(sel_zero, 1)
            idg = w1st[:, IDENT:IDENT + P].rearrange("p (g d) -> p g d", g=G).unsqueeze(2).to_broadcast([P, G, 2, GD])
            v.tensor_copy(sel[:, 0, :, 0:2, :], idg).then_inc(sel_ok, 1)
            v.tensor_copy(sel[:, 1, :, 2:4, :], idg).then_inc(sel_ok, 1)
            normalise_first(0)
            dve.wait_ge(k_ok, 1)
            done(v.tensor_tensor(kf[:].rearrange("p (a g) k -> p a g k", a=2),
                                 k_ps[:, :, 0:2 * B * SK].rearrange("p a (g k) -> p a g k", g=2),
                                 w1st[:, KB:KB + G].rearrange("p (a g) -> p a g", a=2).unsqueeze(3)
                                 .to_broadcast([P, 2, 2, B * SK]), ALU.add))
            done(v.tensor_copy(kpart[:], kf[:]))
            flat = "p g k -> p (g k)"
            v.scalar_tensor_tensor(kpart[:].rearrange(flat), kpart[:].bitcast(F32).rearrange(flat),
                                   w1st[:, KSIGN:KSIGN + 1], kf[:].rearrange(flat),
                                   ALU.mult, ALU.add).then_inc(kpart_ok, 1)
            split_low(0)
            moments(1)
            dve.wait_ge(v_ok, 1)
            dve.wait_ge(cst_in, 16)
            for b in range(B):
                v.tensor_tensor(vtmp[:, b, :], v_ps[0:KR, b, 0:KT * P], cst[0:KR, VMASK:VMASK + KT * P], ALU.mult
                                ).then_inc(v_read, 1)
            v.tensor_tensor(rw_c[:], w2nd[:, RW:RW + E], mean_ps, ALU.subtract).then_inc(rw_ok, 1)
            copy_stack(1)
            normalise_first(1)
            copy_stack(3)
            kb = kpart[:].rearrange("p g (b k) -> p b g k", b=B).bitcast(F32)
            dve.wait_ge(kpart_ok, 1)
            for h in range(HG):
                v.tensor_scalar(kblk[:, 1, :, h * SK:(h + 1) * SK], kb[:, 1], w1st[:, KMASK + h:KMASK + h + 1], None,
                                ALU.mult).then_inc(kblk_ok, 1)
            split_low(1)
            copy_stack(4)
            dve.wait_ge(v_read, B)
            dve.wait_ge(bvm_ok, 1)
            for b in range(B):
                v.tensor_tensor(vblk[:, b].rearrange("p t n -> p (t n)"), vtmp[:, b, :],
                                bvm[:].rearrange("p t n -> p (t n)"), ALU.add).then_inc(vblk_ok, 1)
            for n in range(G + 1, 2 * G):
                copy_stack(n)

            def residual(b):
                for step in range(CB + 1):
                    n = b * CB + step
                    if step < CB:
                        dve.wait_ge(y_ok, n + 1 if b else CB)
                        if step == 0:
                            dve.wait_ge(xb_ok, b + 1)
                        v.tensor_tensor(rows[:, n, 0:D], y_ps[b][step], x_sb[:, n, :], ALU.add).then_inc(x1_ok, 1)
                    if step:
                        dve.wait_ge(x1_ok, n)
                        ins = v.bn_stats(stats[:, n - 1, :], rows[:, n - 1, 0:D])
                done(ins)
                for c in range(CB):
                    n = b * CB + c
                    ins = v.bn_aggr(rows[:, n, MEAN:RSTD + 1], stats[:, n, :])
                ins.then_inc(aggr2_ok, 1)

            def choose(b):
                cs = slice(b * CB, (b + 1) * CB)
                bc = [P, CB, E]
                dve.wait_ge(logit_ok, CB * (b + 1))
                dve.wait_ge(rstd2_ok, b + 1)
                v.tensor_tensor(logit[:, cs, :], logit_ps[b][:, 0:CB * E].rearrange("p (c e) -> p c e", c=CB),
                                rows[:, cs, RSTD:RSTD + 1].to_broadcast(bc), ALU.mult).then_inc(logit_read, 1)
                dve.wait_ge(logit_read, b + 1)
                done(v.tensor_tensor(logit[:, cs, :], logit[:, cs, :],
                                     brow[:, 2 * D:2 * D + E].unsqueeze(1).to_broadcast(bc), ALU.add))
                done(v.tensor_reduce(lmax[:, cs], logit[:, cs, :], AX, ALU.max))
                big = lmax[:, cs].unsqueeze(2).to_broadcast(bc)
                done(v.tensor_tensor(eq[:, cs, :], logit[:, cs, :], big, ALU.is_equal))
                done(v.tensor_tensor(eq[:, cs, :], eq[:, cs, :], cst[:, DESC:DESC + E].unsqueeze(1).to_broadcast(bc), ALU.mult))
                done(v.tensor_reduce(first[:, cs], eq[:, cs, :], AX, ALU.max))
                v.tensor_tensor(chosen[:, cs, :], eq[:, cs, :], first[:, cs].unsqueeze(2).to_broadcast(bc),
                                ALU.is_equal).then_inc(chosen_ok, 1)
                v.tensor_tensor(lsub[:, cs, :], logit[:, cs, :], big, ALU.subtract).then_inc(lsub_ok, 1)

            def probability(b):
                cs = slice(b * CB, (b + 1) * CB)
                dve.wait_ge(sig_ok, 2 * (b + 1))
                done(v.reciprocal(lexp[:, cs, :], sig[:, 1, cs, :]))
                done(v.tensor_tensor(lexp[:, cs, :], lexp[:, cs, :], sig[:, 0, cs, :], ALU.mult))
                done(v.tensor_reduce(lsum[:, cs], lexp[:, cs, :], AX, ALU.add))
                v.reciprocal(rows[:, cs, PROB], lsum[:, cs]).then_inc(prob_row_ok, 1)

            def open_tiles(b):
                dve.wait_ge(rank_ok, b + 1)
                done(v.tensor_tensor(over[:], count_ps[b].unsqueeze(2).to_broadcast([P, E, NX]),
                                     cst[:, THRESH:THRESH + NX].unsqueeze(1).to_broadcast([P, E, NX]), ALU.is_gt))
                done(v.tensor_reduce(extra[:, b, :], over[:], AX, ALU.add))
                if b:
                    done(v.tensor_tensor(extra[:, 1, :], extra[:, 1, :], extra[:, 0, :], ALU.subtract))
                done(v.tensor_tensor(before[:], extra[:, b, :].unsqueeze(1).to_broadcast([P, E, E]),
                                     cst[:, TRI:TRI + E * E].rearrange("p (e f) -> p e f", e=E), ALU.mult))
                done(v.tensor_reduce(opened[:, b, :], before[:], AX, ALU.add))

            base4 = cst[:, BASE:BASE + E].unsqueeze(1).to_broadcast([P, CB, E])

            def give_slots(b):
                cs = slice(b * CB, (b + 1) * CB)
                bc = [P, CB, E]
                s8 = slot8[:, cs, :]
                done(v.scalar_tensor_tensor(s8, rank_ps[b], P - 0.5, jump[:, 0, :].unsqueeze(1).to_broadcast(bc),
                                            ALU.is_gt, ALU.mult))
                if b:
                    done(v.tensor_tensor(late[:], rank_ps[b], thresh1[:].unsqueeze(1).to_broadcast(bc), ALU.is_gt))
                    done(v.tensor_tensor(late[:], late[:], jump[:, 1, :].unsqueeze(1).to_broadcast(bc), ALU.mult))
                    done(v.tensor_tensor(s8, s8, late[:], ALU.add))
                v.tensor_tensor(s8, s8, rank_ps[b], ALU.add).then_inc(rank_read, 1)
                dve.wait_ge(rank_read, b + 1)
                done(v.tensor_tensor(s8, s8, base4, ALU.add))
                done(v.tensor_tensor(s8, s8, chosen[:, cs, :], ALU.mult))
                done(v.tensor_reduce(slotf[:, cs], s8, AX, ALU.add))
                v.tensor_copy(slot[:, cs], slotf[:, cs]).then_inc(slot_ok, 1)

            residual(0)
            choose(0)
            open_tiles(0)
            done(v.scalar_tensor_tensor(jump[:, 0, :], opened[:, 0, :], float(P), cst[:, JUMP:JUMP + E], ALU.mult, ALU.add))
            give_slots(0)
            probability(0)
            v.tensor_tensor(upto[:, 0, :], opened[0:1, 0, :], extra[0:1, 0, :], ALU.add)
            done(v.tensor_tensor(total[:], opened[:, 0, E - 1:E], extra[:, 0, E - 1:E], ALU.add))
            done(v.tensor_tensor(opened[:, 0, :], opened[:, 0, :], extra[:, 0, :], ALU.add))
            v.tensor_scalar(thresh1[:], extra[:, 0, :], float(P), P - 0.5, ALU.mult, ALU.add)
            done(v.tensor_scalar(opened[:, 0, :], opened[:, 0, :], total[:], -1.0, ALU.subtract, ALU.mult))
            residual(1)
            choose(1)
            open_tiles(1)
            done(v.tensor_tensor(jump[:, 1, :], opened[:, 1, :], opened[:, 0, :], ALU.add))
            done(v.tensor_scalar(jump[:, 1, :], jump[:, 1, :], float(P), None, ALU.mult))
            give_slots(1)
            probability(1)
            done(v.tensor_tensor(upto[:, 1, :], opened[0:1, 1, :], extra[0:1, 1, :], ALU.add))
            done(v.tensor_scalar(upto[:, 1, :], upto[:, 1, :], total[0:1, :], None, ALU.add))
            done(v.tensor_tensor(cmp_t[:], upto[:].unsqueeze(2).to_broadcast([1, B, NX, E]),
                                 cst[0:1, TILE_NO:TILE_NO + NX].unsqueeze(1).unsqueeze(3).to_broadcast([1, B, NX, E]), ALU.is_le))
            done(v.tensor_reduce(owner_f[:], cmp_t[:], AX, ALU.add))
            done(v.scalar_tensor_tensor(owner_s[:], owner_f[:, 0, :], E - 0.5, owner_f[:, 0, :], ALU.is_lt, ALU.mult))
            done(v.tensor_tensor(owner_s[:], owner_s[:], owner_f[:, 1, :], ALU.add))
            v.tensor_scalar(owner[:], owner_s[:], float(E - 1), None, ALU.min).then_inc(owner_ok, 1)

            def normalise(i):
                for n, (a, z) in enumerate(srow_parts):
                    if i == a:
                        dve.wait_ge(srow_in[n], 16)
                v.tensor_scalar(sxn[:, i, :], srow[:, i, 0:D], srow[:, i, MEAN:MEAN + 1], srow[:, i, RSTD:RSTD + 1],
                                ALU.subtract, ALU.mult).then_inc(sxn_ok, 1)

            def copy_T(i):
                dve.wait_ge(sT_ok, i + 1)
                v.tensor_copy(sxnT[:, i, :], t_ps[i % 2][:, 0:P]).then_inc(sT_copied, 1)

            def finish(i):
                dve.wait_ge(f_ok, i + 1)
                if i == 0:
                    dve.wait_ge(b2_in, 16)
                if i == E:
                    dve.wait_ge(wx_in, 32 * NX)
                v.tensor_tensor(y_sb[:, i, :], f_ps[i % 2][:, 0:D], b2_sb[:, i, :], ALU.add).then_inc(f_read, 1)
                dve.wait_ge(f_read, i + 1)
                v.scalar_tensor_tensor(o_sb[:, i, :], y_sb[:, i, :], srow[:, i, PROB:PROB + 1], srow[:, i, 0:D],
                                       ALU.mult, ALU.add).then_inc(o_ok, 1)

            for i in range(LEAD):
                normalise(i)
            for i in range(AHEAD):
                copy_T(i)
                normalise(i + LEAD)
            for i in range(NT):
                if i + AHEAD < NT:
                    copy_T(i + AHEAD)
                if i + AHEAD + LEAD < NT:
                    normalise(i + AHEAD + LEAD)
                finish(i)

        @block.scalar
        def _(act):
            a = nc.scalar
            act.dma_start(w1st[:], w_first).then_inc(first_in, 16)
            act.wait_ge(half_ok, 1)
            a.activation(warm[:, 0:1], half[:, 0:1], ACT.Sigmoid)
            act.wait_ge(first_in, 16)
            a.copy(wkrep[:], w1st[:, KW:KW + D].rearrange("p (g d) -> p g d", g=G).unsqueeze(2).to_broadcast([P, G, 4, GD])
                   ).then_inc(wkrep_ok, 1)
            for b in range(B):
                a.copy(ctxrep[:, b, 0:HG * SK].rearrange("p (h k) -> p h k", h=HG),
                       w1st[:, CTX + b * SK:CTX + (b + 1) * SK].unsqueeze(1).to_broadcast([P, HG, SK])).then_inc(ctxrep_ok, 1)

            def copy_xT(b):
                act.wait_ge(xT_ok, b + 1)
                a.copy(xnT[:, b, :], xT_ps[b][:]).then_inc(xT_copied, 1)

            def split_high(b):
                act.wait_ge(q_ok, b + 1)
                a.activation(q_part[:, b, 0, :], q_ps[:], ACT.Identity, bias=w1st[:, QB:QB + 1]).then_inc(qhi_ok, 1)

            def copy_stack(n):
                act.wait_ge(stack_ok, n + 1)
                a.copy(q_stack[:, n // G, n % G, :], stack_ps[n % 2][:]).then_inc(stacked[n % 2], 1)

            def sigmoid(n):
                b, t, pr = units[n]
                act.wait_ge(score_ok, n + 1)
                a.activation(probs[:, b, t, 2 * pr:2 * pr + 2, :], pair[n % 2][0:KR, :, :], ACT.Sigmoid,
                             scale=float(DH) ** -0.5).then_inc(prob_ok, 1)

            def copy_attention(b):
                act.wait_ge(att_ok, b + 1)
                for c in range(CB):
                    a.copy(attT[:, b, c * P:(c + 1) * P], att_ps[b][:, c * P:(c + 1) * P]).then_inc(att_copied, 1)

            def copy_x1T(b):
                for c in range(CB):
                    n = b * CB + c
                    act.wait_ge(x1T_ok, n + 1 if b else CB)
                    a.copy(xnT[:, b, c * P:(c + 1) * P], x1T_ps[b][c]).then_inc(x1T_copied, 1)

            def router_sigmoids(b):
                cs = slice(b * CB, (b + 1) * CB)
                act.wait_ge(lsub_ok, b + 1)
                for k, sign in enumerate((1.0, -1.0)):
                    a.activation(sig[:, k, cs, :], lsub[:, cs, :], ACT.Sigmoid, scale=sign).then_inc(sig_ok, 1)

            copy_xT(0)
            split_high(0)
            kb = kpart[:].rearrange("p g (b k) -> p b g k", b=B).bitcast(F32)
            act.wait_ge(kpart_ok, 1)
            for h in range(HG):
                a.activation(kblk[:, 0, :, h * SK:(h + 1) * SK], kb[:, 0], ACT.Copy,
                             scale=w1st[:, KMASK + h:KMASK + h + 1]).then_inc(kblk_ok, 1)
            copy_stack(ACT_STACKS[0])
            for n in range(len(units)):
                sigmoid(n)
                if n == 0:
                    copy_stack(ACT_STACKS[1])
                if n == 1:
                    copy_xT(1)
                if n == 2:
                    split_high(1)
                if n == 7:
                    copy_attention(0)
                if n == 9:
                    copy_x1T(0)
            router_sigmoids(0)
            copy_attention(1)
            copy_x1T(1)
            router_sigmoids(1)
            a.activation(warm[:, 1:2], half[:, 0:1], ACT.Gelu_apprx_tanh)
            for i in range(NT):
                act.wait_ge(h_ok, i + 1)
                if i >= 3:
                    act.wait_ge(f_ok, i - 2)
                if i == E:
                    act.wait_ge(wx_in, 32 * NX)
                for k in range(FC):
                    a.activation(hT[:, i % 3, k * P:(k + 1) * P], h_ps[i % 2][:, k * P:(k + 1) * P], ACT.Gelu_apprx_tanh,
                                 bias=w_sb[:, i, WB + k:WB + k + 1]).then_inc(gelu_ok, 1)

        @block.tensor
        def _(pe):
            mm, tr = nc.tensor.matmul, nc.tensor.transpose
            ident = w1st[:, IDENT:IDENT + P]
            ones_bf = tri_bf[:, P:2 * P]

            def all_stacked(last):
                for par in range(2):
                    if (n := (last + 2 - par) // 2) > 0:
                        pe.wait_ge(stacked[par], n)

            def transpose_x(b):
                for c in range(CB):
                    pe.wait_ge(xn_ok, b * CB + c + 1)
                    ins = tr(xT_ps[b][:, c * P:(c + 1) * P], xn[:, b * CB + c, :], ident)
                ins.then_inc(xT_ok, 1)

            def project_q(b):
                pe.wait_ge(xT_copied, b + 1)
                pe.wait_ge(second_in, 16)
                if b:
                    pe.wait_ge(qlo_ok, b)
                mm(q_ps[:], w2nd[:, QW:QW + D], xnT[:, b, :], start=True, stop=True).then_inc(q_ok, 1)

            def stack_q(n):
                b, g = n // G, n % G
                if g == 0:
                    pe.wait_ge(qlo_ok, b + 1)
                if n == 0:
                    pe.wait_ge(sel_ok, 2)
                if n >= 2:
                    pe.wait_ge(stacked[n % 2], n // 2)
                for k in range(2):
                    ins = mm(stack_ps[n % 2][:], sel[:, k, g].rearrange("p r d -> p (r d)"), q_part[:, b, k, :],
                             start=(k == 0), stop=(k == 1))
                ins.then_inc(stack_ok, 1)

            def score(n):
                b, t, pr = units[n]
                if n == 0:
                    pe.wait_ge(kblk_ok, 1 + HG)
                if b and units[n - 1][0] == 0:
                    pe.wait_ge(kblk_ok, 1 + HG * B)
                if n == 1:
                    pe.wait_ge(v_read, B)
                    pe.wait_ge(rw_ok, 1)
                if n >= 2:
                    pe.wait_ge(prob_ok, n - 1)
                for j in range(2):
                    g = 2 * pr + j
                    all_stacked(b * G + g)
                    ins = mm(pair[n % 2][0:KR, j, :], kblk[:, b, g, t * KR:(t + 1) * KR], q_stack[:, b, g, :],
                             start=True, stop=True)
                ins.then_inc(score_ok, 1)

            def attend(b, t):
                pe.wait_ge(prob_ok, ATT_AFTER[b, t])
                if t == 0:
                    pe.wait_ge(vblk_ok, B)
                    pe.wait_ge([xT_copied, qlo_ok][b], B)
                for g in range(G):
                    ins = mm(att_ps[b][g * GD:(g + 1) * GD, :], vblk[:, b, t, g * GD:(g + 1) * GD],
                             probs[:, b, t, g, :], start=(t == 0), stop=(t == KT - 1))
                if t == KT - 1:
                    ins.then_inc(att_ok, 1)

            def project_out(b, cs):
                for c in cs:
                    if b == 0:
                        all_stacked(2 * G - 1)
                    else:
                        (rank_held, x1T_held, logit_held, score_held)[c]()
                    pe.wait_ge(att_copied, b * CB + c + 1)
                    mm(y_ps[b][c], attT[:, b, c * P:(c + 1) * P], w2nd[:, OW:OW + D], start=True, stop=True
                       ).then_inc(y_ok, 1)

            def rank_held():
                pe.wait_ge(rank_read, 1)

            def x1T_held():
                pe.wait_ge(x1T_copied, CB)

            def logit_held():
                pe.wait_ge(logit_read, 1)

            def score_held():
                pe.wait_ge(prob_ok, len(units))

            def transpose_x1(b, cs):
                for c in cs:
                    n = b * CB + c
                    if b:
                        score_held()
                        if c == 3:
                            pe.wait_ge(x1_ok, CB + 1)
                    else:
                        all_stacked(2 * G - 1)
                    pe.wait_ge(x1_ok, n + 1)
                    tr(x1T_ps[b][c], rows[:, n, 0:D], ident).then_inc(x1T_ok, 1)

            def router(b, cs):
                for c in cs:
                    n = b * CB + c
                    if c == 0:
                        pe.wait_ge(rw_ok, 1)
                        if b == 0:
                            pe.wait_ge(att_copied, CB)
                        else:
                            pe.wait_ge(x1_ok, CB + 2)
                    pe.wait_ge(x1T_copied, n + 1)
                    mm(logit_ps[b][:, c * E:(c + 1) * E], xnT[:, b, c * P:(c + 1) * P], rw_c[:], start=True, stop=True
                       ).then_inc(logit_ok, 1)

            def rank(b):
                pe.wait_ge(chosen_ok, b + 1)
                pe.wait_ge(tri_ok, 2)
                pe.wait_ge(x1_ok, CB * (b + 1))
                ch = chosen[:].rearrange("p c e -> p (c e)")
                at, w = b * CB * E, CB * E
                acc = rank_bank[b]
                mm(acc[:, 0:w], tri_bf[:, 0:P], ch[:, at:at + w], start=True, stop=False, skip_group_check=True)
                for s in range(1, CB):
                    mm(acc[:, s * E:w], ones_bf, ch[:, at:at + w - s * E], start=False, stop=False, skip_group_check=True)
                if b:
                    for c in range(CB):
                        mm(rank_ps[b], ones_bf, chosen[:, c, :].unsqueeze(1).to_broadcast([P, CB, E]), start=False,
                           stop=False, skip_group_check=True)
                for c in range((b + 1) * CB):
                    ins = mm(count_ps[b], ones_bf, chosen[:, c, :], start=False, stop=(c == (b + 1) * CB - 1),
                             skip_group_check=True)
                ins.then_inc(rank_ok, 1)

            every = range(CB)
            pe.wait_ge(first_in, 16)
            pe.wait_ge(wkrep_ok, 1)
            for g in range(G):
                ins = mm(k_ps[:, g // 2, (g % 2) * B * SK:(g % 2 + 1) * B * SK], wkrep[:, g].rearrange("p r d -> p (r d)"),
                         w1st[:, CTX:CTX + B * SK], start=True, stop=True)
            ins.then_inc(k_ok, 1)
            transpose_x(0)

            def project_v(b):
                for t in range(KT):
                    ins = mm(v_ps[0:KR, b, t * P:(t + 1) * P], ctxrep[:, b, t * KR:(t + 1) * KR], w2nd[:, VW:VW + D],
                             start=True, stop=True)
                return ins

            pe.wait_ge(ctxrep_ok, B + 1)
            pe.wait_ge(second_in, 16)
            project_v(0)
            project_q(0)
            project_v(1)
            pe.wait_ge(ones_ok, 1)
            mm(mean_ps, mean_w[:], w2nd[:, RW:RW + E], start=True, stop=True).then_inc(v_ok, 1)
            stack_q(0)
            stack_q(1)
            score(0)
            stack_q(2)
            stack_q(3)
            score(1)
            transpose_x(1)
            score(2)
            project_q(1)
            score(3)
            stack_q(4)
            stack_q(5)
            score(4)
            stack_q(6)
            score(5)
            attend(0, 0)
            stack_q(7)
            score(6)
            attend(0, 1)
            score(7)
            attend(0, 2)
            score(8)
            score(9)
            project_out(0, every)
            attend(1, 0)
            score(10)
            transpose_x1(0, every)
            score(11)
            attend(1, 1)
            router(0, every)
            rank(0)
            attend(1, 2)
            project_out(1, every)
            for step in range(CB + 1):
                if step < CB:
                    transpose_x1(1, [step])
                if step:
                    router(1, [step - 1])
            rank(1)

            def transpose_slots(i):
                pe.wait_ge(sxn_ok, i + 1)
                if i >= 2:
                    pe.wait_ge(sT_copied, i - 1)
                tr(t_ps[i % 2][:, 0:P], sxn[:, i, :], ident).then_inc(sT_ok, 1)

            def up(i):
                pe.wait_ge(sT_copied, i + 1)
                if i == 0:
                    pe.wait_ge(w_in, 16 * E // 2)
                if i == E:
                    pe.wait_ge(wx_in, 32 * NX)
                if i >= 2:
                    pe.wait_ge(gelu_ok, FC * (i - 1))
                for k in range(FC):
                    ins = mm(h_ps[i % 2][:, k * P:(k + 1) * P], w_sb[:, i, W1 + k * P:W1 + (k + 1) * P], sxnT[:, i, :],
                             start=True, stop=True)
                ins.then_inc(h_ok, 1)

            def down(i):
                if i >= 2:
                    pe.wait_ge(f_read, i - 1)
                for k in range(FC):
                    pe.wait_ge(gelu_ok, FC * i + k + 1)
                    ins = mm(f_ps[i % 2][:, 0:D], hT[:, i % 3, k * P:(k + 1) * P], w_sb[:, i, W2 + k * D:W2 + (k + 1) * D],
                             start=(k == 0), stop=(k == FC - 1))
                ins.then_inc(f_ok, 1)

            for i in range(AHEAD):
                transpose_slots(i)
            for i in range(NT):
                up(i)
                if i + AHEAD < NT:
                    transpose_slots(i + AHEAD)
                if i >= 1:
                    down(i - 1)
            down(NT - 1)


def kernel(x, ctx_1024, L0_xattn_Wq, L0_xattn_bq, L0_xattn_Wk, L0_xattn_bk, L0_xattn_Wv, L0_xattn_bv, L0_xattn_Wo,
           L0_xattn_bo, L0_ffn_switch_w, L0_ffn_switch_b, L0_ffn_w1, L0_ffn_b1, L0_ffn_w2, L0_ffn_b2):
    import concourse.bacc as bacc
    from concourse.bass_utils import run_bass_kernel_spmd

    a = np.asarray
    cat = np.concatenate
    w1, w2, b1 = a(L0_ffn_w1), a(L0_ffn_w2), a(L0_ffn_b1)
    arrays = {
        "tokens": a(x).reshape(NTOK, D),
        "w_first": cat([a(L0_xattn_Wk).T, np.tile(a(L0_xattn_bk).reshape(G, 1, GD), (1, 4, 1)).reshape(G, P).T,
                        a(L0_xattn_bq).reshape(D, 1), first_constants(), a(ctx_1024).reshape(B * SK, D).T], axis=1),
        "w_second": cat([a(L0_xattn_Wq).T, a(L0_xattn_Wv).T, a(L0_xattn_Wo).T, a(L0_ffn_switch_w)], axis=1),
        "bias_row": cat([a(L0_xattn_bv), a(L0_xattn_bo), a(L0_ffn_switch_b)]).reshape(1, 2 * D + E),
        "const": constants(),
        "weights": cat([w1, w2.reshape(E, FC, P, D).transpose(0, 2, 1, 3).reshape(E, P, F),
                        b1.reshape(E, FC, P).transpose(0, 2, 1)], axis=2),
        "b2": a(L0_ffn_b2),
    }
    arrays = {k: np.ascontiguousarray(v) for k, v in arrays.items()}
    nc = bacc.Bacc("TRN2", target_bir_lowering=False, num_devices=1)
    aps = [nc.dram_tensor(k, v.shape, mybir.dt.from_np(v.dtype), kind="ExternalInput").ap() for k, v in arrays.items()]
    out = nc.dram_tensor("result", (NTOK, D), mybir.dt.float32, kind="ExternalOutput").ap()
    build_program(nc, *aps, out)
    r = run_bass_kernel_spmd(nc, [arrays], core_ids=[0])
    return r.results[0]["result"].reshape(B, S, D)
```

```python
from contextlib import ExitStack

import numpy as np

import concourse.bass as bass
from concourse import mybir

P = 128
B, S, D = 2, 512, 128
SK = 77
H, DH = 16, 8
E, F = 8, 512
NTOK = B * S
C = NTOK // P
CB = S // P
G = 4
GD = D // G
HG = H // G
KT = 3
KR = -(-HG * SK // KT)
KC = KT * KR
FC = F // P
NX = C - 1
NT = E + NX
W1, W2 = 0, F
WB = 2 * F
WCOLS = 2 * F + FC
MEAN, RSTD, PROB, TOK = D, D + 1, D + 2, D + 3
ROW = D + 4
EPS = 1e-5
DIRECT = 4
AHEAD = 2
LEAD = 3

KW, KB, QB, IDENT = 0, D, D + G, D + G + 1
KMASK = IDENT + P
KSIGN = KMASK + HG
CTX = KSIGN + 1
NFIRST = CTX + B * SK
QW, VW, OW, RW = 0, D, 2 * D, 3 * D
NSECOND = 3 * D + E
VMASK = 0
DESC = VMASK + KT * P
TRI = DESC + E
JUMP = TRI + E * E
BASE = JUMP + E
TILE_NO = BASE + E
NCONST = TILE_NO + NX
TILES_PER = (1 - 2.0 ** -12) / P
ROUND = 1.5 * 2.0 ** 23


def first_constants():
    p = np.arange(P)
    t = np.zeros((P, P + HG + 1), np.float32)
    t[:, 0:P] = np.eye(P)
    for h in range(HG):
        t[:, P + h] = (p % GD) // DH == h
    t[:, P + HG] = -((p // GD) % 2)
    return t


def constants():
    t = np.zeros((P, NCONST), np.float32)
    p = np.arange(P)
    for k in range(KT):
        for r in range(KR):
            key = k * KR + r
            if key < HG * SK:
                t[r, VMASK + k * P:VMASK + (k + 1) * P] = (p % GD) // DH == key // SK
    e = np.arange(E)
    t[:, DESC:DESC + E] = E - e
    t[:, TRI:TRI + E * E] = P * (e[None, :] < e[:, None]).reshape(-1)
    t[:, JUMP:JUMP + E] = (E - 1) * P - P * e
    t[:, BASE:BASE + E] = P * e
    t[:, TILE_NO:TILE_NO + NX] = P * np.arange(NX)
    return t


def build_program(nc, x, w_first, w_second, rows_1, const, weights, b2, out):
    F32, F32R, BF16, I32 = mybir.dt.float32, mybir.dt.float32r, mybir.dt.bfloat16, mybir.dt.int32
    ALU, ACT, AX = mybir.AluOpType, mybir.ActivationFunctionType, mybir.AxisListType.X
    ctx = ExitStack()
    with ctx:
        def sb(name, shape, dt=F32):
            return ctx.enter_context(nc.sbuf_tensor(name, shape, dt))

        def sem(name):
            return ctx.enter_context(nc.semaphore(name))

        x_sb = sb("x_sb", [P, C, D])
        w1st = sb("w1st", [P, NFIRST])
        w2nd = sb("w2nd", [P, NSECOND])
        cst = sb("cst", [P, NCONST])
        brow = sb("brow", [P, 2 * D + E])
        wkrep = sb("wkrep", [P, G, 4, GD])
        ctxrep = sb("ctxrep", [P, B, KC])
        bvm = sb("bvm", [KR, KT, P])
        sel = sb("sel", [P, 2, G, 4, GD], F32R)
        tri_bf = sb("tri_bf", [P, 2 * P], BF16)
        heat = sb("heat", [P, 512], BF16)
        mean_w = sb("mean_w", [P, P])
        rw_c = sb("rw_c", [P, E])
        half = sb("half", [P, C])
        warm = sb("warm", [P, 2])
        stats = sb("stats", [P, C, 6])
        ln1 = sb("ln1", [P, C, 2])
        var_eps = sb("var_eps", [P, C])
        rstd1 = sb("rstd1", [P, C])
        xn = sb("xn", [P, C, D])
        xnT = sb("xnT", [P, B, S])
        q_part = sb("q_part", [P, B, 2, S], F32R)
        q_stack = sb("q_stack", [P, B, G, S], F32R)
        kf = sb("kf", [P, G, B * SK])
        kpart = sb("kpart", [P, G, B * SK], F32R)
        kblk = sb("kblk", [P, B, G, KC], F32R)
        vtmp = sb("vtmp", [KR, B, KT * P])
        vblk = sb("vblk", [KR, B, KT, P])
        attT = sb("attT", [P, B, S])
        rows = sb("rows", [P, C, ROW])
        logit = sb("logit", [P, C, E])
        lmax = sb("lmax", [P, C])
        lsub = sb("lsub", [P, C, E])
        sig = sb("sig", [P, 2, C, E])
        lexp = sb("lexp", [P, C, E])
        lsum = sb("lsum", [P, C])
        eq = sb("eq", [P, C, E])
        first = sb("first", [P, C])
        chosen = sb("chosen", [P, C, E], BF16)
        rounded = sb("rounded", [P, B, E])
        extra = sb("extra", [P, B, E])
        before = sb("before", [P, E, E])
        opened = sb("opened", [P, B, E])
        total = sb("total", [P, 1])
        jump = sb("jump", [P, B, E])
        thresh1 = sb("thresh1", [P, E])
        round1 = sb("round1", [P, E])
        adjust = sb("adjust", [P, E])
        slot8 = sb("slot8", [P, C, E])
        late = sb("late", [P, CB, E])
        slotf = sb("slotf", [P, C])
        slot = sb("slot", [P, C], I32)
        slot_no = sb("slot_no", [P, DIRECT * P])
        slot_no_i = sb("slot_no_i", [P, DIRECT * P], I32)
        shift2 = sb("shift2", [P, C])
        upto = sb("upto", [1, B, E])
        cmp_t = sb("cmp_t", [1, B, NX, E])
        owner_f = sb("owner_f", [1, B, NX])
        owner_s = sb("owner_s", [1, NX])
        owner = sb("owner", [1, NX], I32)
        blank = sb("blank", [P, ROW])
        shared = sb("shared", [P, B * KT * G * S])
        probs = shared[0:KR, :].rearrange("p (b t g s) -> p b t g s", b=B, t=KT, g=G)
        srow, sxn, sxnT, y_sb, o_sb = (
            shared[:, NT * at:NT * (at + n)].rearrange("p (i n) -> p i n", i=NT)
            for at, n in ((0, ROW), (ROW, D), (ROW + D, P), (ROW + D + P, D), (ROW + 2 * D + P, D)))
        hT = shared[:, NT * (ROW + 3 * D + P):NT * (ROW + 3 * D + P) + 3 * F].rearrange("p (i n) -> p i n", i=3)
        x1n, x1_part = xn, q_part[:, 0]
        one_hot = q_stack[:].rearrange("p b g s -> p (b g) s")
        w_sb = sb("w_sb", [P, NT, WCOLS])
        b2_sb = sb("b2_sb", [P, NT, D])

        pair = [ctx.enter_context(nc.psum_tensor(f"pair{i}", [P, 2, 512], F32)) for i in range(2)]
        bank = [ctx.enter_context(nc.psum_tensor(f"bank{i}", [P, 512], F32)) for i in range(4)]
        k_ps, v_ps = pair
        xT_ps = [bank[0], bank[1]]
        stack_ps = [bank[0], bank[3]]
        q_pieces = [[(bank[2][:, 0:S // 2], slice(0, S // 2)), (bank[3][:, 0:S // 2], slice(S // 2, S))],
                    [(bank[2][:], slice(0, S))]]
        att_ps = [bank[1], bank[2]]
        y_ps = [[bank[0][:, c * D:(c + 1) * D] for c in range(CB)],
                [t[:, 0:D] for t in (bank[3], bank[1], pair[0][:, 0, :], pair[0][:, 1, :])]]
        x1T_ps = [[bank[3][:, c * P:(c + 1) * P] for c in range(CB)],
                  [t[:, 0:P] for t in (pair[1][:, 0, :], pair[1][:, 1, :], bank[3], bank[1])]]
        logit_ps = [bank[1], bank[2]]
        rank_bank = [bank[0], pair[0][:, 0, :]]
        rank_ps = [t[:, 0:CB * E].rearrange("p (c e) -> p c e", c=CB) for t in rank_bank]
        count_ps = [t[:, CB * E:CB * E + E] for t in rank_bank]
        mean_ps = pair[1][:, 1, KT * P:KT * P + E]
        h_ps = [pair[1][:, 0, :], pair[1][:, 1, :]]
        direct_ps = bank[0][:, 0:DIRECT * P]
        t_ps = [bank[0], bank[1]]
        f_ps = [bank[2], bank[3]]

        slots_dram = nc.dram_tensor("slots_dram", (NT * P, ROW), F32).ap()

        x_in = [sem(f"x_in{b}") for b in range(B)]
        first_in, second_in, cst_in, brow_in = sem("first_in"), sem("second_in"), sem("cst_in"), sem("brow_in")
        w_in, b2_in = sem("w_in"), sem("b2_in")
        wx_in = [sem(f"wx_in{i}") for i in range(NX)]
        slot_no_ok, shift2_ok, x1n_ok, x1_high_ok = sem("slot_no_ok"), sem("shift2_ok"), sem("x1n_ok"), sem("x1_high_ok")
        x1_low_ok, one_hot_ok, direct_ok, direct_copied = (sem("x1_low_ok"), sem("one_hot_ok"), sem("direct_ok"),
                                                           sem("direct_copied"))
        blank_ok, blanked, stored = sem("blank_ok"), sem("blanked"), sem("stored")
        sent = [sem("sent"), sem("sent_last")]
        srow_in = [sem(f"srow_in{i}") for i in range(3)]
        pool_step, dve_step = sem("pool_step"), sem("dve_step")
        half_ok, heat_ok, ones_ok, sel_zero, tok_ok = (sem("half_ok"), sem("heat_ok"), sem("ones_ok"), sem("sel_zero"),
                                                       sem("tok_ok"))
        wkrep_ok, ctxrep_ok, bvm_ok, tri_ok, sel_ok = (sem("wkrep_ok"), sem("ctxrep_ok"), sem("bvm_ok"),
                                                       sem("tri_ok"), sem("sel_ok"))
        rw_ok = sem("rw_ok")
        aggr_ok, rstd_ok, xn_ok, xT_ok, xT_copied = (sem("aggr_ok"), sem("rstd_ok"), sem("xn_ok"),
                                                     sem("xT_ok"), sem("xT_copied"))
        xb_ok = sem("xb_ok")
        k_ok, kpart_ok, kblk_ok, v_ok, v_read, vblk_ok = (sem("k_ok"), sem("kpart_ok"), sem("kblk_ok"),
                                                          sem("v_ok"), sem("v_read"), sem("vblk_ok"))
        q_ok, qhi_ok, qlo_ok, stack_ok = sem("q_ok"), sem("qhi_ok"), sem("qlo_ok"), sem("stack_ok")
        stacked = [sem(f"stacked{i}") for i in range(2)]
        score_ok, prob_ok, att_ok, att_copied = sem("score_ok"), sem("prob_ok"), sem("att_ok"), sem("att_copied")
        y_ok, x1_ok, x1_late_ok, aggr2_ok, rstd2_ok = (sem("y_ok"), sem("x1_ok"), sem("x1_late_ok"), sem("aggr2_ok"),
                                                       sem("rstd2_ok"))
        x1T_ok, x1T_copied, logit_ok, logit_read = sem("x1T_ok"), sem("x1T_copied"), sem("logit_ok"), sem("logit_read")
        lsub_ok, sig_ok, chosen_ok, rank_ok, rank_read = (sem("lsub_ok"), sem("sig_ok"), sem("chosen_ok"),
                                                          sem("rank_ok"), sem("rank_read"))
        slot_ok, owner_ok, prob_row_ok = sem("slot_ok"), sem("owner_ok"), sem("prob_row_ok")
        sxn_ok, sT_ok, sT_copied, h_ok, gelu_ok, f_ok, f_read, o_ok = (
            sem("sxn_ok"), sem("sT_ok"), sem("sT_copied"), sem("h_ok"), sem("gelu_ok"), sem("f_ok"),
            sem("f_read"), sem("o_ok"))

        units = [(0, t, pr) for pr in range(2) for t in range(KT)] + [(1, t, pr) for t in range(KT) for pr in range(2)]
        ATT_AFTER = {(b, t): 1 + max(n for n, u in enumerate(units) if u[:2] == (b, t)) for b in range(B) for t in range(KT)}
        ACT_STACKS = (0, 2)
        BY_PE = (2, 3)
        srow_parts = [(DIRECT, DIRECT + LEAD), (0, DIRECT), (DIRECT + LEAD, NT)]

        def pieces_done(b):
            return sum(len(pieces) for pieces in q_pieces[0:b + 1])

        def x1_written(engine, n):
            engine.wait_ge(x1_ok, min(n + 1, CB + BY_PE[0]))
            if n >= CB + BY_PE[0]:
                engine.wait_ge(x1_late_ok, n + 1 - CB - BY_PE[0])

        block = ctx.enter_context(nc.Block())

        @block.sync
        def _(sp):
            xv = x.rearrange("(c p) d -> p c d", p=P)
            sp.dma_start(x_sb[:, 0:CB, :], xv[:, 0:CB, :]).then_inc(x_in[0], 16)
            sp.dma_start(x_sb[:, CB:C, :], xv[:, CB:C, :]).then_inc(x_in[1], 16)
            sp.dma_start(w2nd[:], w_second).then_inc(second_in, 16)
            sp.dma_start(cst[:], const).then_inc(cst_in, 16)
            sp.dma_start(brow[:], rows_1.to_broadcast([P, 2 * D + E])).then_inc(brow_in, 16)
            sp.wait_ge(blank_ok, 2)
            sp.dma_start(slots_dram.rearrange("(n p) r -> p n r", p=P), blank[:].unsqueeze(1).to_broadcast([P, NT, ROW])
                         ).then_inc(blanked, 16)
            for e in range(0, E, 2):
                sp.dma_start(w_sb[:, e:e + 2, :], weights[e:e + 2].rearrange("e p n -> p e n")).then_inc(w_in, 16)
            sp.dma_start(b2_sb[:, 0:E, :], b2.rearrange("e d -> (e d)").unsqueeze(0).to_broadcast([P, E * D])
                         .rearrange("p (e d) -> p e d", e=E)).then_inc(b2_in, 16)
            sp.wait_ge(sent[0], 16 * (CB + 1))
            sp.wait_ge(sent[1], 16 * (CB - 1))
            for i, (a, z) in enumerate(srow_parts):
                sp.dma_start(srow[:, a:z, :], slots_dram[a * P:z * P, :].rearrange("(n p) r -> p n r", p=P)
                             ).then_inc(srow_in[i], 16)
            sp.wait_ge(owner_ok, 1)
            for i in range(NX):
                e = sp.value_load(owner[0:1, i:i + 1], min_val=0, max_val=E - 1)
                sp.dma_start(w_sb[:, E + i, :], weights[bass.ds(e, 1)].rearrange("e p n -> p (e n)")).then_inc(wx_in[i], 16)
                sp.dma_start(b2_sb[:, E + i, :], b2[bass.ds(e, 1)].to_broadcast([P, D])).then_inc(wx_in[i], 16)

        @block.gpsimd
        def _(pool):
            gp = nc.gpsimd
            gp.memset(heat[:], -0.5).then_inc(heat_ok, 1)
            gp.memset(half[:], -0.5).then_inc(half_ok, 1)
            gp.memset(ctxrep[:, :, HG * SK:KC], 0.0).then_inc(ctxrep_ok, 1)
            gp.memset(sel[:].bitcast(F32), 0.0).then_inc(sel_zero, 1)
            gp.memset(blank[:], 0.0).then_inc(blank_ok, 1)
            pool.wait_ge(blank_ok, 1)
            gp.memset(blank[:, TOK:TOK + 1].bitcast(I32), NTOK).then_inc(blank_ok, 1)
            gp.iota(rows[:, :, TOK:TOK + 1].bitcast(I32).rearrange("p c o -> p (c o)"), pattern=[[P, C]], base=0,
                    channel_multiplier=1).then_inc(tok_ok, 1)
            gp.memset(mean_w[:], 1.0 / D).then_inc(ones_ok, 1)
            gp.memset(kblk[:, :, :, HG * SK:KC].bitcast(F32), 0.0).then_inc(kblk_ok, 1)
            gp.memset(tri_bf[:], 1.0).then_inc(tri_ok, 1)

            for b in range(B):
                cs = slice(b * CB, (b + 1) * CB)
                pool.wait_ge(aggr_ok, b + 1)
                gp.tensor_scalar(var_eps[:, cs], ln1[:, cs, 1], EPS, None, ALU.add).then_inc(pool_step, 1)
                pool.wait_ge(pool_step, b + 1)
                if b == 0:
                    pool.wait_ge(half_ok, 1)
                gp.tensor_tensor(rstd1[:, cs], var_eps[:, cs], half[:, cs], ALU.pow).then_inc(rstd_ok, 1)
            pool.wait_ge(tri_ok, 1)
            gp.affine_select(out=tri_bf[:, 0:P], in_=tri_bf[:, 0:P], compare_op=ALU.is_gt, fill=0.0, base=0,
                             pattern=[[1, P]], channel_multiplier=-1).then_inc(tri_ok, 1)
            pool.wait_ge(brow_in, 16)
            pool.wait_ge(cst_in, 16)
            gp.tensor_tensor(bvm[:], cst[0:KR, VMASK:VMASK + KT * P].rearrange("p (t n) -> p t n", t=KT),
                             brow[0:KR, 0:D].unsqueeze(1).to_broadcast([KR, KT, P]), ALU.mult).then_inc(bvm_ok, 1)
            for b in range(B):
                cs = slice(b * CB, (b + 1) * CB)
                pool.wait_ge(xn_ok, (b + 1) * CB)
                gp.tensor_tensor(x_sb[:, cs, :], x_sb[:, cs, :], brow[:, D:2 * D].unsqueeze(1).to_broadcast([P, CB, D]),
                                 ALU.add).then_inc(xb_ok, 1)
            gp.iota(slot_no_i[:], pattern=[[1, DIRECT * P]], base=0, channel_multiplier=0).then_inc(slot_no_ok, 1)
            pool.wait_ge(slot_no_ok, 1)
            gp.tensor_copy(slot_no[:], slot_no_i[:]).then_inc(slot_no_ok, 1)
            for n in range(C // 2):
                cs = slice(2 * n, 2 * n + 2)
                pool.wait_ge(aggr2_ok, n + 1)
                gp.tensor_scalar(var_eps[:, cs], rows[:, cs, RSTD], EPS, None, ALU.add).then_inc(pool_step, 1)
                pool.wait_ge(pool_step, B + n + 1)
                gp.tensor_tensor(rows[:, cs, RSTD], var_eps[:, cs], half[:, cs], ALU.pow).then_inc(rstd2_ok, 1)
            pool.wait_ge(blanked, 16)
            pool.wait_ge(tok_ok, 1)
            for b in range(B):
                pool.wait_ge(rstd2_ok, (b + 1) * CB // 2)
                pool.wait_ge(prob_row_ok, b + 1)
                pool.wait_ge(slot_ok, b + 1)
                for c in range(b * CB, (b + 1) * CB):
                    gp.indirect_dma_start(slots_dram, bass.IndirectOffsetOnAxis(ap=slot[:, c:c + 1], axis=0),
                                          rows[:, c, :], None, bounds_check=NT * P - 1, oob_is_err=False
                                          ).then_inc(sent[c > CB], 16)
            for i in range(NT):
                pool.wait_ge(o_ok, i + 1)
                gp.indirect_dma_start(out, bass.IndirectOffsetOnAxis(ap=srow[:, i, TOK:TOK + 1].bitcast(I32), axis=0),
                                      o_sb[:, i, :], None, bounds_check=NTOK - 1, oob_is_err=False).then_inc(stored, 16)
            pool.wait_ge(stored, 16 * NT)

        @block.vector
        def _(dve):
            v = nc.vector
            steps = [0]

            def note(ins):
                steps[0] += 1
                ins.then_inc(dve_step, 1)
                return steps[0]

            def need(step):
                dve.wait_ge(dve_step, step)

            def done(ins):
                need(note(ins))

            def normalise_first(b):
                dve.wait_ge(rstd_ok, b + 1)
                for c in range(b * CB, (b + 1) * CB):
                    v.tensor_scalar(xn[:, c, :], x_sb[:, c, :], ln1[:, c, 0:1], rstd1[:, c:c + 1],
                                    ALU.subtract, ALU.mult).then_inc(xn_ok, 1)

            def moments(b):
                dve.wait_ge(x_in[b], 16)
                for c in range(b * CB, (b + 1) * CB):
                    ins = v.bn_stats(stats[:, c, :], x_sb[:, c, :])
                done(ins)
                for c in range(b * CB, (b + 1) * CB):
                    ins = v.bn_aggr(ln1[:, c, :], stats[:, c, :])
                ins.then_inc(aggr_ok, 1)

            def split_low(b):
                for i, (acc, at) in enumerate(q_pieces[b]):
                    dve.wait_ge(qhi_ok, pieces_done(b - 1) + i + 1)
                    v.scalar_tensor_tensor(q_part[:, b, 1, at], acc, w1st[:, QB:QB + 1], q_part[:, b, 0, at].bitcast(F32),
                                           ALU.add, ALU.subtract).then_inc(qlo_ok, 1)

            def copy_stack(n):
                dve.wait_ge(stack_ok, n + 1)
                v.tensor_copy(q_stack[:, n // G, n % G, :], stack_ps[n % 2][:]).then_inc(stacked[n % 2], 1)

            moments(0)
            dve.wait_ge(first_in, 16)
            dve.wait_ge(sel_zero, 1)
            idg = w1st[:, IDENT:IDENT + P].rearrange("p (g d) -> p g d", g=G).unsqueeze(2).to_broadcast([P, G, 2, GD])
            v.tensor_copy(sel[:, 0, :, 0:2, :], idg).then_inc(sel_ok, 1)
            v.tensor_copy(sel[:, 1, :, 2:4, :], idg).then_inc(sel_ok, 1)
            moments(1)
            normalise_first(0)
            dve.wait_ge(k_ok, 1)
            done(v.tensor_tensor(kf[:].rearrange("p (a g) k -> p a g k", a=2),
                                 k_ps[:, :, 0:2 * B * SK].rearrange("p a (g k) -> p a g k", g=2),
                                 w1st[:, KB:KB + G].rearrange("p (a g) -> p a g", a=2).unsqueeze(3)
                                 .to_broadcast([P, 2, 2, B * SK]), ALU.add))
            done(v.tensor_copy(kpart[:], kf[:]))
            flat = "p g k -> p (g k)"
            v.scalar_tensor_tensor(kpart[:].rearrange(flat), kpart[:].bitcast(F32).rearrange(flat),
                                   w1st[:, KSIGN:KSIGN + 1], kf[:].rearrange(flat),
                                   ALU.mult, ALU.add).then_inc(kpart_ok, 1)
            kb = kpart[:].rearrange("p g (b k) -> p b g k", b=B).bitcast(F32)

            def mask_keys(b, heads):
                dve.wait_ge(kpart_ok, 1)
                for h in heads:
                    v.tensor_scalar(kblk[:, b, :, h * SK:(h + 1) * SK], kb[:, b], w1st[:, KMASK + h:KMASK + h + 1], None,
                                    ALU.mult).then_inc(kblk_ok, 1)

            mask_keys(0, range(0, HG // 2))
            split_low(0)
            mask_keys(0, range(HG // 2, HG))
            copy_stack(1)
            dve.wait_ge(v_ok, 1)
            dve.wait_ge(cst_in, 16)
            for b in range(B):
                v.tensor_tensor(vtmp[:, b, :], v_ps[0:KR, b, 0:KT * P], cst[0:KR, VMASK:VMASK + KT * P], ALU.mult
                                ).then_inc(v_read, 1)
            v.tensor_tensor(rw_c[:], w2nd[:, RW:RW + E], mean_ps, ALU.subtract).then_inc(rw_ok, 1)
            normalise_first(1)

            def add_value_bias(b):
                dve.wait_ge(v_read, B)
                dve.wait_ge(bvm_ok, 1)
                v.tensor_tensor(vblk[:, b].rearrange("p t n -> p (t n)"), vtmp[:, b, :],
                                bvm[:].rearrange("p t n -> p (t n)"), ALU.add).then_inc(vblk_ok, 1)

            add_value_bias(0)
            dve.wait_ge(xT_ok, B)
            v.tensor_copy(xnT[:, 1, :], xT_ps[1][:]).then_inc(xT_copied, 1)
            copy_stack(3)
            mask_keys(1, range(HG))
            split_low(1)
            add_value_bias(1)
            copy_stack(4)
            for n in range(G + 1, 2 * G):
                copy_stack(n)

            def add_residual(n):
                dve.wait_ge(y_ok, max(n + 1, CB))
                dve.wait_ge(xb_ok, n // CB + 1)
                v.tensor_tensor(rows[:, n, 0:D], y_ps[n // CB][n % CB], x_sb[:, n, :], ALU.add).then_inc(x1_ok, 1)

            def x1_stats(n):
                x1_written(dve, n)
                return v.bn_stats(stats[:, n, :], rows[:, n, 0:D])

            def x1_moments(n):
                for m in (n, n + 1):
                    ins = v.bn_aggr(rows[:, m, MEAN:RSTD + 1], stats[:, m, :])
                ins.then_inc(aggr2_ok, 1)

            bc = [P, CB, E]
            rows_of = [slice(b * CB, (b + 1) * CB) for b in range(B)]

            def choose(b):
                cs = rows_of[b]
                dve.wait_ge(logit_ok, CB * (b + 1))
                dve.wait_ge(rstd2_ok, (b + 1) * CB // 2)
                v.tensor_tensor(logit[:, cs, :], logit_ps[b][:, 0:CB * E].rearrange("p (c e) -> p c e", c=CB),
                                rows[:, cs, RSTD:RSTD + 1].to_broadcast(bc), ALU.mult).then_inc(logit_read, 1)
                dve.wait_ge(logit_read, b + 1)
                done(v.tensor_tensor(logit[:, cs, :], logit[:, cs, :],
                                     brow[:, 2 * D:2 * D + E].unsqueeze(1).to_broadcast(bc), ALU.add))
                done(v.tensor_reduce(lmax[:, cs], logit[:, cs, :], AX, ALU.max))
                big = lmax[:, cs].unsqueeze(2).to_broadcast(bc)
                store_shift(b)
                is_big = note(v.tensor_tensor(eq[:, cs, :], logit[:, cs, :], big, ALU.is_equal))
                v.tensor_tensor(lsub[:, cs, :], logit[:, cs, :], big, ALU.subtract).then_inc(lsub_ok, 1)
                need(is_big)
                done(v.tensor_tensor(eq[:, cs, :], eq[:, cs, :], cst[:, DESC:DESC + E].unsqueeze(1).to_broadcast(bc), ALU.mult))
                done(v.tensor_reduce(first[:, cs], eq[:, cs, :], AX, ALU.max))
                v.tensor_tensor(chosen[:, cs, :], eq[:, cs, :], first[:, cs].unsqueeze(2).to_broadcast(bc),
                                ALU.is_equal).then_inc(chosen_ok, 1)

            def prob_reciprocal(b):
                dve.wait_ge(sig_ok, 2 * (b + 1))
                return note(v.reciprocal(lexp[:, rows_of[b], :], sig[:, 1, rows_of[b], :]))

            def prob_exp(b):
                cs = rows_of[b]
                return note(v.tensor_tensor(lexp[:, cs, :], lexp[:, cs, :], sig[:, 0, cs, :], ALU.mult))

            def prob_sum(b):
                return note(v.tensor_reduce(lsum[:, rows_of[b]], lexp[:, rows_of[b], :], AX, ALU.add))

            def prob_store(b):
                v.reciprocal(rows[:, rows_of[b], PROB], lsum[:, rows_of[b]]).then_inc(prob_row_ok, 1)

            def tiles_before(b):
                return note(v.scalar_tensor_tensor(
                    before[:], rounded[:, b, :].unsqueeze(1).to_broadcast([P, E, E]), ROUND,
                    cst[:, TRI:TRI + E * E].rearrange("p (e f) -> p e f", e=E), ALU.subtract, ALU.mult))

            def sum_before(b):
                return note(v.tensor_reduce(opened[:, b, :], before[:], AX, ALU.add))

            def in_slots(b):
                return note(v.tensor_scalar(extra[:, b, :], rounded[:, b, :], ROUND, float(P), ALU.subtract, ALU.mult))

            def store_slots(b, s8):
                with nc.allow_low_precision(reason="slot numbers are whole and small"):
                    v.tensor_reduce(slot[:, rows_of[b]], s8, AX, ALU.add).then_inc(slot_ok, 1)

            def float_slots(b):
                return note(v.tensor_reduce(slotf[:, rows_of[b]], slot8[:, rows_of[b], :], AX, ALU.add))

            def store_shift(b):
                cs = rows_of[b]
                v.scalar_tensor_tensor(shift2[:, cs], rows[:, cs, MEAN], -1.0, rows[:, cs, RSTD], ALU.mult, ALU.mult
                                       ).then_inc(shift2_ok, 1)

            def low_part():
                dve.wait_ge(x1_high_ok, 1)
                v.tensor_tensor(x1_part[:, 1, :], x1n[:, rows_of[1], :].rearrange("p c d -> p (c d)"),
                                x1_part[:, 0, :].bitcast(F32), ALU.subtract).then_inc(x1_low_ok, 1)

            def mark_slots(n):
                if n == 0:
                    dve.wait_ge(slot_no_ok, 2)
                v.tensor_scalar(one_hot[:, n, 0:DIRECT * P], slot_no[:], slotf[:, n:n + 1], None, ALU.is_equal).then_inc(one_hot_ok, 1)

            base4 = cst[:, BASE:BASE + E].unsqueeze(1).to_broadcast(bc)

            dve.wait_ge(att_ok, 1)
            for c in range(CB):
                v.tensor_copy(attT[:, 0, c * P:(c + 1) * P], att_ps[0][:, c * P:(c + 1) * P]).then_inc(att_copied, 1)
            add_residual(0)
            add_residual(1)
            x1_stats(0)
            pair_ok = note(x1_stats(1))
            add_residual(2)
            add_residual(3)
            need(pair_ok)
            x1_moments(0)
            x1_stats(2)
            done(x1_stats(3))
            x1_moments(2)
            for c in range(CB):
                dve.wait_ge(x1T_ok, CB)
                v.tensor_copy(xnT[:, 0, c * P:(c + 1) * P], x1T_ps[0][c]).then_inc(x1T_copied, 1)
            choose(0)
            s8 = slot8[:, rows_of[0], :]
            need(prob_reciprocal(0))
            prob_exp(0)
            dve.wait_ge(rank_ok, 1)
            step = note(v.tensor_scalar(rounded[:, 0, :], count_ps[0], TILES_PER, ROUND, ALU.mult, ALU.add))
            note(v.tensor_tensor(s8, rank_ps[0], base4, ALU.add))
            need(step)
            step = tiles_before(0)
            need(step)
            step = sum_before(0)
            v.scalar_tensor_tensor(late[:], rank_ps[0], P - 0.5, chosen[:, rows_of[0], :], ALU.is_gt, ALU.mult
                                   ).then_inc(rank_read, 1)
            need(step)
            step = note(v.tensor_tensor(jump[:, 0, :], opened[:, 0, :], cst[:, JUMP:JUMP + E], ALU.add))
            note(v.tensor_tensor(s8, s8, chosen[:, rows_of[0], :], ALU.mult))
            add_residual(CB)
            dve.wait_ge(rank_read, 1)
            need(step)
            step = note(v.tensor_tensor(late[:], late[:], jump[:, 0, :].unsqueeze(1).to_broadcast(bc), ALU.mult))
            add_residual(CB + 1)
            need(step)
            step = note(v.tensor_tensor(s8, s8, late[:], ALU.add))
            x1_stats(CB)
            need(step)
            store_slots(0, s8)
            pair_ok = note(x1_stats(CB + 1))
            x1_stats(CB + 2)
            need(pair_ok)
            x1_moments(CB)
            pair_ok = note(x1_stats(CB + 3))
            sum_ok = prob_sum(0)
            need(pair_ok)
            x1_moments(CB + 2)
            need(sum_ok)
            prob_store(0)
            slots0_ok = float_slots(0)
            need(in_slots(0))
            v.tensor_scalar(thresh1[:], extra[:, 0, :], P - 0.5, None, ALU.add)
            note(v.tensor_tensor(total[:], opened[:, 0, E - 1:E], extra[:, 0, E - 1:E], ALU.add))
            note(v.tensor_tensor(adjust[:], opened[:, 0, :], extra[:, 0, :], ALU.add))
            step = note(v.tensor_scalar(round1[:], extra[:, 0, :], -1.0 / P, ROUND, ALU.mult, ALU.add))
            need(step)
            v.tensor_copy(upto[:, 0, :], adjust[0:1, :])
            step = note(v.tensor_scalar(opened[:, 0, :], adjust[:], total[:], -1.0, ALU.subtract, ALU.mult))
            need(slots0_ok)
            for n in range(CB - 2):
                mark_slots(n)
            choose(1)
            cs = rows_of[1]
            s8 = slot8[:, cs, :]
            need(prob_reciprocal(1))
            prob_exp(1)
            mark_slots(CB - 2)
            dve.wait_ge(rank_ok, 2)
            step = note(v.scalar_tensor_tensor(rounded[:, 1, :], count_ps[1], TILES_PER, round1[:], ALU.mult, ALU.add))
            is_late = note(v.tensor_tensor(late[:], rank_ps[1], thresh1[:].unsqueeze(1).to_broadcast(bc), ALU.is_gt))
            need(step)
            step = tiles_before(1)
            s_ok = note(v.scalar_tensor_tensor(s8, rank_ps[1], P - 0.5, jump[:, 0, :].unsqueeze(1).to_broadcast(bc),
                                               ALU.is_gt, ALU.mult))
            need(step)
            step = sum_before(1)
            need(s_ok)
            s_ok = note(v.tensor_tensor(s8, s8, rank_ps[1], ALU.add))
            need(step)
            step = note(v.tensor_tensor(jump[:, 1, :], opened[:, 1, :], opened[:, 0, :], ALU.add))
            is_late = note(v.tensor_tensor(late[:], late[:], chosen[:, cs, :], ALU.mult))
            need(s_ok)
            s_ok = note(v.tensor_tensor(s8, s8, base4, ALU.add))
            need(is_late)
            step = note(v.tensor_tensor(late[:], late[:], jump[:, 1, :].unsqueeze(1).to_broadcast(bc), ALU.mult))
            need(s_ok)
            s_ok = note(v.tensor_tensor(s8, s8, chosen[:, cs, :], ALU.mult))
            sum_ok = prob_sum(1)
            need(s_ok)
            step = note(v.tensor_tensor(s8, s8, late[:], ALU.add))
            need(sum_ok)
            prob_store(1)
            need(step)
            store_slots(1, s8)
            slots1_ok = float_slots(1)
            mark_slots(CB - 1)
            low_part()
            need(slots1_ok)
            for n in range(CB, C):
                mark_slots(n)
            need(in_slots(1))
            done(v.tensor_tensor(upto[:, 1, :], opened[0:1, 1, :], extra[0:1, 1, :], ALU.add))
            done(v.tensor_scalar(upto[:, 1, :], upto[:, 1, :], total[0:1, :], None, ALU.add))
            done(v.tensor_tensor(cmp_t[:], upto[:].unsqueeze(2).to_broadcast([1, B, NX, E]),
                                 cst[0:1, TILE_NO:TILE_NO + NX].unsqueeze(1).unsqueeze(3).to_broadcast([1, B, NX, E]), ALU.is_le))
            done(v.tensor_reduce(owner_f[:], cmp_t[:], AX, ALU.add))
            done(v.scalar_tensor_tensor(owner_s[:], owner_f[:, 0, :], E - 0.5, owner_f[:, 0, :], ALU.is_lt, ALU.mult))
            done(v.tensor_tensor(owner_s[:], owner_s[:], owner_f[:, 1, :], ALU.add))
            v.tensor_scalar(owner[:], owner_s[:], float(E - 1), None, ALU.min).then_inc(owner_ok, 1)

            def srow_arrived(i):
                for n, (a, z) in enumerate(srow_parts):
                    if i == a:
                        dve.wait_ge(srow_in[n], 16)

            def normalise(i):
                srow_arrived(i)
                v.tensor_scalar(sxn[:, i, :], srow[:, i, 0:D], srow[:, i, MEAN:MEAN + 1], srow[:, i, RSTD:RSTD + 1],
                                ALU.subtract, ALU.mult).then_inc(sxn_ok, 1)

            def copy_T(i):
                dve.wait_ge(sT_ok, i - DIRECT + 1)
                v.tensor_copy(sxnT[:, i, :], t_ps[i % 2][:, 0:P]).then_inc(sT_copied, 1)

            def add_b2(i):
                dve.wait_ge(f_ok, i + 1)
                if i == 0:
                    dve.wait_ge(b2_in, 16)
                if i >= E:
                    dve.wait_ge(wx_in[i - E], 32)
                v.tensor_tensor(y_sb[:, i, :], f_ps[i % 2][:, 0:D], b2_sb[:, i, :], ALU.add).then_inc(f_read, 1)

            def finish(i):
                if i < DIRECT:
                    srow_arrived(i)
                dve.wait_ge(f_read, i + 1)
                v.scalar_tensor_tensor(o_sb[:, i, :], y_sb[:, i, :], srow[:, i, PROB:PROB + 1], srow[:, i, 0:D],
                                       ALU.mult, ALU.add).then_inc(o_ok, 1)

            for i in range(DIRECT - 2):
                add_b2(i)
            for i in range(DIRECT, DIRECT + LEAD):
                normalise(i)
            copy_T(DIRECT)
            add_b2(DIRECT - 2)
            for i in range(1, AHEAD):
                copy_T(DIRECT + i)
            for i in range(DIRECT - 1):
                finish(i)
            for i in range(DIRECT - 1, NT):
                if i >= DIRECT and i + AHEAD < NT:
                    copy_T(i + AHEAD)
                if i + 1 + LEAD < NT:
                    normalise(i + 1 + LEAD)
                add_b2(i)
                finish(i)

        @block.scalar
        def _(act):
            a = nc.scalar
            act.dma_start(w1st[:], w_first).then_inc(first_in, 16)
            act.wait_ge(half_ok, 1)
            a.activation(warm[:, 0:1], half[:, 0:1], ACT.Sigmoid)
            act.wait_ge(first_in, 16)
            a.copy(wkrep[:], w1st[:, KW:KW + D].rearrange("p (g d) -> p g d", g=G).unsqueeze(2).to_broadcast([P, G, 4, GD])
                   ).then_inc(wkrep_ok, 1)
            for b in range(B):
                a.copy(ctxrep[:, b, 0:HG * SK].rearrange("p (h k) -> p h k", h=HG),
                       w1st[:, CTX + b * SK:CTX + (b + 1) * SK].unsqueeze(1).to_broadcast([P, HG, SK])).then_inc(ctxrep_ok, 1)

            def split_high(b):
                for i, (acc, at) in enumerate(q_pieces[b]):
                    act.wait_ge(q_ok, pieces_done(b - 1) + i + 1)
                    a.activation(q_part[:, b, 0, at], acc, ACT.Identity, bias=w1st[:, QB:QB + 1]).then_inc(qhi_ok, 1)

            def copy_stack(n):
                act.wait_ge(stack_ok, n + 1)
                a.copy(q_stack[:, n // G, n % G, :], stack_ps[n % 2][:]).then_inc(stacked[n % 2], 1)

            def sigmoid(n):
                b, t, pr = units[n]
                act.wait_ge(score_ok, n + 1)
                a.activation(probs[:, b, t, 2 * pr:2 * pr + 2, :], pair[n % 2][0:KR, :, :], ACT.Sigmoid,
                             scale=float(DH) ** -0.5).then_inc(prob_ok, 1)

            def copy_x1T(b):
                for c in range(CB):
                    act.wait_ge(x1T_ok, b * CB + c + 1)
                    a.copy(xnT[:, b, c * P:(c + 1) * P], x1T_ps[b][c]).then_inc(x1T_copied, 1)

            def router_sigmoids(b):
                cs = slice(b * CB, (b + 1) * CB)
                act.wait_ge(lsub_ok, b + 1)
                for k, sign in enumerate((1.0, -1.0)):
                    a.activation(sig[:, k, cs, :], lsub[:, cs, :], ACT.Sigmoid, scale=sign).then_inc(sig_ok, 1)

            act.wait_ge(xT_ok, 1)
            a.copy(xnT[:, 0, :], xT_ps[0][:]).then_inc(xT_copied, 1)
            split_high(0)
            copy_stack(ACT_STACKS[0])
            for n in range(len(units)):
                sigmoid(n)
                if n == 0:
                    copy_stack(ACT_STACKS[1])
                if n == 2:
                    split_high(1)

            def normalise_x1(b):
                act.wait_ge(shift2_ok, b + 1)
                for n in range(b * CB, (b + 1) * CB):
                    a.activation(x1n[:, n, :], rows[:, n, 0:D], ACT.Identity, scale=rows[:, n, RSTD:RSTD + 1],
                                 bias=shift2[:, n:n + 1]).then_inc(x1n_ok, 1)

            router_sigmoids(0)
            act.wait_ge(att_ok, B)
            for c in range(CB):
                a.copy(attT[:, 1, c * P:(c + 1) * P], att_ps[1][:, c * P:(c + 1) * P]).then_inc(att_copied, 1)
            for c in BY_PE:
                act.wait_ge(y_ok, CB + c + 1)
                a.copy(rows[:, CB + c, 0:D], y_ps[1][c]).then_inc(x1_late_ok, 1)
            copy_x1T(1)
            normalise_x1(0)
            router_sigmoids(1)
            normalise_x1(1)
            act.wait_ge(x1n_ok, C)
            a.activation(x1_part[:, 0, :], x1n[:, CB:C, :].rearrange("p c d -> p (c d)"), ACT.Copy).then_inc(x1_high_ok, 1)
            a.activation(warm[:, 1:2], half[:, 0:1], ACT.Gelu_apprx_tanh)
            act.wait_ge(direct_ok, 1)
            for i in range(DIRECT):
                a.copy(sxnT[:, i, :], direct_ps[:, i * P:(i + 1) * P]).then_inc(direct_copied, 1)
            for i in range(NT):
                act.wait_ge(h_ok, i + 1)
                if i >= 3:
                    act.wait_ge(f_ok, i - 2)
                if i >= E:
                    act.wait_ge(wx_in[i - E], 32)
                for k in range(FC):
                    a.activation(hT[:, i % 3, k * P:(k + 1) * P], h_ps[i % 2][:, k * P:(k + 1) * P], ACT.Gelu_apprx_tanh,
                                 bias=w_sb[:, i, WB + k:WB + k + 1]).then_inc(gelu_ok, 1)

        @block.tensor
        def _(pe):
            mm, tr = nc.tensor.matmul, nc.tensor.transpose
            ident = w1st[:, IDENT:IDENT + P]
            ones_bf = tri_bf[:, P:2 * P]

            def all_stacked(last):
                for par in range(2):
                    if (n := (last + 2 - par) // 2) > 0:
                        pe.wait_ge(stacked[par], n)

            def transpose_x(b):
                for c in range(CB):
                    pe.wait_ge(xn_ok, b * CB + c + 1)
                    ins = tr(xT_ps[b][:, c * P:(c + 1) * P], xn[:, b * CB + c, :], ident)
                ins.then_inc(xT_ok, 1)

            def project_q(b):
                pe.wait_ge(xT_copied, b + 1)
                pe.wait_ge(second_in, 16)
                if b:
                    pe.wait_ge(qlo_ok, pieces_done(0))
                for acc, at in q_pieces[b]:
                    mm(acc, w2nd[:, QW:QW + D], xnT[:, b, at], start=True, stop=True).then_inc(q_ok, 1)

            def stack_q(n):
                b, g = n // G, n % G
                if g == 0:
                    pe.wait_ge(qlo_ok, pieces_done(b))
                if n == 0:
                    pe.wait_ge(sel_ok, 2)
                if n >= 2:
                    pe.wait_ge(stacked[n % 2], n // 2)
                for k in range(2):
                    ins = mm(stack_ps[n % 2][:], sel[:, k, g].rearrange("p r d -> p (r d)"), q_part[:, b, k, :],
                             start=(k == 0), stop=(k == 1))
                ins.then_inc(stack_ok, 1)

            def score(n):
                b, t, pr = units[n]
                if n == 0:
                    pe.wait_ge(kblk_ok, 1 + HG)
                if b and units[n - 1][0] == 0:
                    pe.wait_ge(kblk_ok, 1 + HG * B)
                if n == 1:
                    pe.wait_ge(v_read, B)
                    pe.wait_ge(rw_ok, 1)
                if n >= 2:
                    pe.wait_ge(prob_ok, n - 1)
                for j in range(2):
                    g = 2 * pr + j
                    all_stacked(b * G + g)
                    ins = mm(pair[n % 2][0:KR, j, :], kblk[:, b, g, t * KR:(t + 1) * KR], q_stack[:, b, g, :],
                             start=True, stop=True)
                ins.then_inc(score_ok, 1)

            def attend(b, t):
                pe.wait_ge(prob_ok, ATT_AFTER[b, t])
                if t == 0:
                    pe.wait_ge(vblk_ok, b + 1)
                    pe.wait_ge([xT_copied, qlo_ok][b], [B, pieces_done(1)][b])
                for g in range(G):
                    ins = mm(att_ps[b][g * GD:(g + 1) * GD, :], vblk[:, b, t, g * GD:(g + 1) * GD],
                             probs[:, b, t, g, :], start=(t == 0), stop=(t == KT - 1))
                if t == KT - 1:
                    ins.then_inc(att_ok, 1)

            def project_out(b, cs):
                for c in cs:
                    if b == 0:
                        all_stacked(2 * G - 1)
                    elif c not in BY_PE:
                        (x1T_held, logit_held)[c]()
                    pe.wait_ge(att_copied, b * CB + c + 1)
                    mm(y_ps[b][c], attT[:, b, c * P:(c + 1) * P], w2nd[:, OW:OW + D], start=not (b and c in BY_PE), stop=True
                       ).then_inc(y_ok, 1)

            def start_residual(cs):
                for c in cs:
                    score_held()
                    pe.wait_ge(xb_ok, B)
                    mm(y_ps[1][c], ident, x_sb[:, CB + c, :], start=True, stop=False)

            def x1T_held():
                pe.wait_ge(x1T_copied, CB)

            def logit_held():
                pe.wait_ge(logit_read, 1)

            def score_held():
                pe.wait_ge(prob_ok, len(units))

            def transpose_x1(b, cs):
                for c in cs:
                    n = b * CB + c
                    if b:
                        score_held()
                        if c >= 2:
                            x1_written(pe, CB + c - 2)
                    else:
                        all_stacked(2 * G - 1)
                    x1_written(pe, n)
                    tr(x1T_ps[b][c], rows[:, n, 0:D], ident).then_inc(x1T_ok, 1)

            def router(b, cs):
                for c in cs:
                    n = b * CB + c
                    if c == 0:
                        pe.wait_ge(rw_ok, 1)
                        if b == 0:
                            pe.wait_ge(att_copied, CB)
                        else:
                            pe.wait_ge(att_copied, 2 * CB)
                    pe.wait_ge(x1T_copied, n + 1)
                    mm(logit_ps[b][:, c * E:(c + 1) * E], xnT[:, b, c * P:(c + 1) * P], rw_c[:], start=True, stop=True
                       ).then_inc(logit_ok, 1)

            def rank(b):
                pe.wait_ge(chosen_ok, b + 1)
                pe.wait_ge(tri_ok, 2)
                pe.wait_ge(heat_ok, 1)
                x1_written(pe, CB * (b + 1) - 1)
                ch = chosen[:].rearrange("p c e -> p (c e)")
                at, w = b * CB * E, CB * E
                acc = rank_bank[b]
                mm(acc[:, 0:w], tri_bf[:, 0:P], ch[:, at:at + w], start=True, stop=False, skip_group_check=True)
                for s in range(1, CB):
                    mm(acc[:, s * E:w], ones_bf, ch[:, at:at + w - s * E], start=False, stop=False, skip_group_check=True)
                if b:
                    for c in range(CB):
                        mm(rank_ps[b], ones_bf, chosen[:, c, :].unsqueeze(1).to_broadcast([P, CB, E]), start=False,
                           stop=False, skip_group_check=True)
                mm(count_ps[b], ones_bf, heat[:, 0:E], start=False, stop=False, skip_group_check=True)
                for c in range((b + 1) * CB):
                    ins = mm(count_ps[b], ones_bf, chosen[:, c, :], start=False, stop=(c == (b + 1) * CB - 1),
                             skip_group_check=True)
                ins.then_inc(rank_ok, 1)

            def keep_warm(bank_free, n):
                for _ in range(n):
                    mm(bank_free, heat[:, 0:P], heat[:], start=True, stop=True)

            every = range(CB)
            pe.wait_ge(heat_ok, 1)
            keep_warm(bank[2][:], 9)
            pe.wait_ge(first_in, 16)
            pe.wait_ge(wkrep_ok, 1)
            for g in range(G):
                ins = mm(k_ps[:, g // 2, (g % 2) * B * SK:(g % 2 + 1) * B * SK], wkrep[:, g].rearrange("p r d -> p (r d)"),
                         w1st[:, CTX:CTX + B * SK], start=True, stop=True)
            ins.then_inc(k_ok, 1)

            def project_v(b):
                for t in range(KT):
                    ins = mm(v_ps[0:KR, b, t * P:(t + 1) * P], ctxrep[:, b, t * KR:(t + 1) * KR], w2nd[:, VW:VW + D],
                             start=True, stop=True)
                return ins

            pe.wait_ge(ctxrep_ok, B + 1)
            pe.wait_ge(second_in, 16)
            project_v(0)
            transpose_x(0)
            project_v(1)
            pe.wait_ge(ones_ok, 1)
            mm(mean_ps, mean_w[:], w2nd[:, RW:RW + E], start=True, stop=True).then_inc(v_ok, 1)
            project_q(0)
            keep_warm(bank[1][:], 5)
            stack_q(0)
            stack_q(1)
            score(0)
            stack_q(2)
            score(1)
            transpose_x(1)
            stack_q(3)
            score(2)
            project_q(1)
            score(3)
            score(4)
            stack_q(4)
            score(5)
            stack_q(5)
            attend(0, 0)
            score(6)
            stack_q(6)
            stack_q(7)
            attend(0, 1)
            score(7)
            attend(0, 2)
            score(8)
            score(9)
            project_out(0, every)
            score(10)
            score(11)
            transpose_x1(0, every)
            attend(1, 0)
            router(0, every)
            attend(1, 1)
            attend(1, 2)
            rank(0)
            start_residual(BY_PE)
            project_out(1, every)
            for step in range(CB + 1):
                if step < CB:
                    transpose_x1(1, [step])
                if step:
                    router(1, [step - 1])

            def send_direct(n):
                pe.wait_ge(one_hot_ok, n + 1)
                if n < CB:
                    pe.wait_ge(x1n_ok, n + 1)
                    if n == 0:
                        pe.wait_ge(rank_read, 1)
                    return mm(direct_ps, x1n[:, n, :], one_hot[:, n, 0:DIRECT * P].bitcast(F32), start=(n == 0), stop=False)
                pe.wait_ge(x1_low_ok, 1)
                for k in range(2):
                    ins = mm(direct_ps, x1_part[:, k, (n - CB) * P:(n - CB + 1) * P], one_hot[:, n, 0:DIRECT * P],
                             start=False, stop=(n == C - 1 and k == 1))
                return ins

            keep_warm(bank[3][:], 3)
            send_direct(0)
            rank(1)
            for n in range(1, C):
                ins = send_direct(n)
            ins.then_inc(direct_ok, 1)

            def transpose_slots(i):
                pe.wait_ge(sxn_ok, i - DIRECT + 1)
                if i >= DIRECT + 2:
                    pe.wait_ge(sT_copied, i - DIRECT - 1)
                elif i == DIRECT:
                    pe.wait_ge(direct_copied, DIRECT)
                tr(t_ps[i % 2][:, 0:P], sxn[:, i, :], ident).then_inc(sT_ok, 1)

            def up(i):
                if i < DIRECT:
                    pe.wait_ge(direct_copied, i + 1)
                else:
                    pe.wait_ge(sT_copied, i - DIRECT + 1)
                if i == 0:
                    pe.wait_ge(w_in, 16 * E // 2)
                if i >= E:
                    pe.wait_ge(wx_in[i - E], 32)
                if i >= 2:
                    pe.wait_ge(gelu_ok, FC * (i - 1))
                for k in range(FC):
                    ins = mm(h_ps[i % 2][:, k * P:(k + 1) * P], w_sb[:, i, W1 + k * P:W1 + (k + 1) * P], sxnT[:, i, :],
                             start=True, stop=True)
                ins.then_inc(h_ok, 1)

            def down(i):
                if i >= 2:
                    pe.wait_ge(f_read, i - 1)
                for k in range(FC):
                    pe.wait_ge(gelu_ok, FC * i + k + 1)
                    ins = mm(f_ps[i % 2][:, 0:D], hT[:, i % 3, k * P:(k + 1) * P], w_sb[:, i, W2 + k * D:W2 + (k + 1) * D],
                             start=(k == 0), stop=(k == FC - 1))
                ins.then_inc(f_ok, 1)

            for i in range(NT):
                up(i)
                if i >= DIRECT and i + AHEAD < NT:
                    transpose_slots(i + AHEAD)
                if i == DIRECT - 1:
                    transpose_slots(DIRECT)
                if i >= 1:
                    down(i - 1)
                if i == DIRECT - 1:
                    for j in range(1, AHEAD):
                        transpose_slots(DIRECT + j)
            down(NT - 1)


def kernel(x, ctx_1024, L0_xattn_Wq, L0_xattn_bq, L0_xattn_Wk, L0_xattn_bk, L0_xattn_Wv, L0_xattn_bv, L0_xattn_Wo,
           L0_xattn_bo, L0_ffn_switch_w, L0_ffn_switch_b, L0_ffn_w1, L0_ffn_b1, L0_ffn_w2, L0_ffn_b2):
    import concourse.bacc as bacc
    from concourse.bass_utils import run_bass_kernel_spmd

    a = np.asarray
    cat = np.concatenate
    w1, w2, b1 = a(L0_ffn_w1), a(L0_ffn_w2), a(L0_ffn_b1)
    arrays = {
        "tokens": a(x).reshape(NTOK, D),
        "w_first": cat([a(L0_xattn_Wk).T, np.tile(a(L0_xattn_bk).reshape(G, 1, GD), (1, 4, 1)).reshape(G, P).T,
                        a(L0_xattn_bq).reshape(D, 1), first_constants(), a(ctx_1024).reshape(B * SK, D).T], axis=1),
        "w_second": cat([a(L0_xattn_Wq).T, a(L0_xattn_Wv).T, a(L0_xattn_Wo).T, a(L0_ffn_switch_w)], axis=1),
        "bias_row": cat([a(L0_xattn_bv), a(L0_xattn_bo), a(L0_ffn_switch_b)]).reshape(1, 2 * D + E),
        "const": constants(),
        "weights": cat([w1, w2.reshape(E, FC, P, D).transpose(0, 2, 1, 3).reshape(E, P, F),
                        b1.reshape(E, FC, P).transpose(0, 2, 1)], axis=2),
        "b2": a(L0_ffn_b2),
    }
    arrays = {k: np.ascontiguousarray(v) for k, v in arrays.items()}
    nc = bacc.Bacc("TRN2", target_bir_lowering=False, num_devices=1)
    aps = [nc.dram_tensor(k, v.shape, mybir.dt.from_np(v.dtype), kind="ExternalInput").ap() for k, v in arrays.items()]
    out = nc.dram_tensor("result", (NTOK, D), mybir.dt.float32, kind="ExternalOutput").ap()
    build_program(nc, *aps, out)
    r = run_bass_kernel_spmd(nc, [arrays], core_ids=[0])
    return r.results[0]["result"].reshape(B, S, D)
```
